# Optimizing a Trainium2 kernel written in Bass

```python
import numpy as np
import jax
import jax.numpy as jnp

def _softmax(x, axis=-1):
    return jax.nn.softmax(x, axis=axis)

def _gelu(x):
    return jax.nn.gelu(x, approximate=True)

def _silu(x):
    return jax.nn.silu(x)

def _sigmoid(x):
    return jax.nn.sigmoid(x)

def _layernorm(x, axis=-1, eps=1e-05):
    m = jnp.mean(x, axis=axis, keepdims=True)
    v = jnp.var(x, axis=axis, keepdims=True)
    return (x - m) / jnp.sqrt(v + eps)

def _scatter_add(tgt, idx, src, axis=0):
    return tgt.at[idx].add(src)

def _segment_sum(src, seg, n):
    return jax.ops.segment_sum(src, seg, n)
kernel_name = 'mk_decoder_preln_d1_seqx_r8_6a9439'

def setup_inputs(seed: int=0):
    np.random.seed(seed)
    _w = jnp.asarray

    def _rec_inputs():
        import jax
        import jax.numpy as jnp
        _rk = jax.random.key(seed)
        x = -0.0002928 + 1 * jax.random.normal(jax.random.fold_in(_rk, 1), (4, 256, 128), jnp.float32)
        _lenS = 256 - jax.random.randint(jax.random.fold_in(_rk, 7), (4,), 0, max(1, 256 // 4) + 1, jnp.int32)
        _lenS2 = 64 - jax.random.randint(jax.random.fold_in(_rk, 8), (4,), 0, max(1, 64 // 4) + 1, jnp.int32)
        _ctx_1024P = jax.random.normal(jax.random.fold_in(_rk, 11), (4, 16, 128), jnp.float32)
        _ctx_1024c = jax.random.dirichlet(jax.random.fold_in(_rk, 511), 0.3 * jnp.ones((16,), jnp.float32), (4, 64))
        _ctx_1024t = jnp.einsum('bsk,bkd->bsd', _ctx_1024c, _ctx_1024P)
        _ctx_1024t = _ctx_1024t * jax.lax.rsqrt(jnp.mean(jnp.square(_ctx_1024t)) + 1e-12) * 0.953939
        ctx_1024 = 4.13588e-05 + 0.999923 * (_ctx_1024t + 0.3 * jax.random.normal(jax.random.fold_in(_rk, 611), (4, 64, 128), jnp.float32))
        return (x, ctx_1024)
    x, ctx_1024 = _rec_inputs()

    def _L0_attn_setup():
        import jax, jax.numpy as jnp
        import numpy as np
        B, T, C = (4, 512, 128)
        H = 16
        LS = 32
        EPS = 1e-06

        def rmsnorm(x, w):
            xf = x.astype(jnp.float32)
            y = xf * jax.lax.rsqrt(jnp.mean(xf * xf, axis=-1, keepdims=True) + EPS)
            return y.astype(x.dtype) * w
        key = jax.random.key(seed)
        k1, k2, k3 = jax.random.split(key, 3)
        x = jax.random.normal(k1, (B, T, C), dtype=jnp.float32)
        w_qkv = jax.random.normal(k2, (C, 3 * C), dtype=jnp.float32) * (1.0 / np.sqrt(C))
        ln_w = jnp.ones((C,), dtype=jnp.float32)
        w_proj = jax.random.normal(k3, (C, C), dtype=jnp.float32) * (1.0 / np.sqrt(C))
        return {'x': x, 'w_qkv': w_qkv, 'ln_w': ln_w, 'w_proj': w_proj}
    _L0_attn_all = _L0_attn_setup()
    _L0_attn_in = {k: v for k, v in _L0_attn_all.items() if k in ('w_qkv', 'ln_w', 'w_proj')}
    del _L0_attn_all

    def _L0_xattn_setup():
        import jax, jax.numpy as jnp
        import numpy as np
        DIM = 128
        NUM_HEADS = 16
        DIM_HEAD = 64
        INNER = NUM_HEADS * DIM_HEAD
        SCALE = DIM_HEAD ** (-0.5)

        def _layernorm(x, gamma, beta, eps=1e-05):
            mu = jnp.mean(x, axis=-1, keepdims=True)
            var = jnp.mean(jnp.square(x - mu), axis=-1, keepdims=True)
            return (x - mu) * jax.lax.rsqrt(var + eps) * gamma + beta
        key = jax.random.key(seed)
        ks = jax.random.split(key, 8)
        B, SQ, SK = (2, 256, 512)
        x = jax.random.normal(ks[0], (B, SQ, DIM), dtype=jnp.float32)
        context = jax.random.normal(ks[1], (B, SK, DIM), dtype=jnp.float32)
        ln_gamma = jnp.ones((DIM,), jnp.float32)
        ln_beta = jnp.zeros((DIM,), jnp.float32)
        w_q = jax.random.normal(ks[2], (DIM, INNER), dtype=jnp.float32) / np.sqrt(DIM)
        w_kv = jax.random.normal(ks[3], (DIM, 2 * INNER), dtype=jnp.float32) / np.sqrt(DIM)
        w_out = jax.random.normal(ks[4], (INNER, DIM), dtype=jnp.float32) / np.sqrt(INNER)
        b_out = jnp.zeros((DIM,), jnp.float32)
        gate = jnp.array([0.5], jnp.float32)
        return {'x': x, 'context': context, 'ln_gamma': ln_gamma, 'ln_beta': ln_beta, 'w_q': w_q, 'w_kv': w_kv, 'w_out': w_out, 'b_out': b_out, 'gate': gate}
    _L0_xattn_all = _L0_xattn_setup()
    _L0_xattn_in = {k: v for k, v in _L0_xattn_all.items() if k in ('ln_gamma', 'ln_beta', 'w_q', 'w_kv', 'w_out', 'b_out', 'gate')}
    del _L0_xattn_all

    def _L0_ffn_setup():
        import jax, jax.numpy as jnp
        import numpy as np
        B, S, D = (1, 256, 128)
        E, F = (16, 128)
        NG, TKG, K = (4, 2, 4)
        NSH = 2
        SCALE = 2.5
        STD = 0.02
        EPG = E // NG

        def _route(x_flat, router_w, bias):
            logits = x_flat.astype(jnp.float32) @ router_w.T
            scores = jax.nn.sigmoid(logits)
            s = scores + bias[None, :]
            sg = s.reshape(-1, NG, EPG)
            group_score = jax.lax.top_k(sg, 2)[0].sum(-1)
            gidx = jax.lax.top_k(group_score, TKG)[1]
            gmask = jnp.sum(jax.nn.one_hot(gidx, NG, dtype=jnp.float32), axis=1) > 0
            emask = jnp.repeat(gmask, EPG, axis=1)
            masked = jnp.where(emask, s, -1.0)
            topk_idx = jax.lax.top_k(masked, K)[1]
            tw = jnp.take_along_axis(scores, topk_idx, axis=1)
            tw = tw / (tw.sum(-1, keepdims=True) + 1e-20)
            tw = tw * SCALE
            return (topk_idx, tw)
        key = jax.random.key(seed)
        ks = jax.random.split(key, 8)
        return {'hidden_states': jax.random.normal(ks[0], (B, S, D), jnp.float32), 'router_w': jax.random.normal(ks[1], (E, D), jnp.float32) * STD, 'bias': jnp.zeros((E,), jnp.float32), 'gate_w': jax.random.normal(ks[2], (E, D, F), jnp.float32) * STD, 'up_w': jax.random.normal(ks[3], (E, D, F), jnp.float32) * STD, 'down_w': jax.random.normal(ks[4], (E, F, D), jnp.float32) * STD, 'sh_gate_w': jax.random.normal(ks[5], (D, NSH * F), jnp.float32) * STD, 'sh_up_w': jax.random.normal(ks[6], (D, NSH * F), jnp.float32) * STD, 'sh_down_w': jax.random.normal(ks[7], (NSH * F, D), jnp.float32) * STD}
    _L0_ffn_all = _L0_ffn_setup()
    _L0_ffn_in = {k: v for k, v in _L0_ffn_all.items() if k in ('router_w', 'bias', 'gate_w', 'up_w', 'down_w', 'sh_gate_w', 'sh_up_w', 'sh_down_w')}
    del _L0_ffn_all
    return {'x': x, 'ctx_1024': ctx_1024, 'L0_attn_w_qkv': _L0_attn_in['w_qkv'], 'L0_attn_ln_w': _L0_attn_in['ln_w'], 'L0_attn_w_proj': _L0_attn_in['w_proj'], 'L0_xattn_ln_gamma': _L0_xattn_in['ln_gamma'], 'L0_xattn_ln_beta': _L0_xattn_in['ln_beta'], 'L0_xattn_w_q': _L0_xattn_in['w_q'], 'L0_xattn_w_kv': _L0_xattn_in['w_kv'], 'L0_xattn_w_out': _L0_xattn_in['w_out'], 'L0_xattn_b_out': _L0_xattn_in['b_out'], 'L0_xattn_gate': _L0_xattn_in['gate'], 'L0_ffn_router_w': _L0_ffn_in['router_w'], 'L0_ffn_bias': _L0_ffn_in['bias'], 'L0_ffn_gate_w': _L0_ffn_in['gate_w'], 'L0_ffn_up_w': _L0_ffn_in['up_w'], 'L0_ffn_down_w': _L0_ffn_in['down_w'], 'L0_ffn_sh_gate_w': _L0_ffn_in['sh_gate_w'], 'L0_ffn_sh_up_w': _L0_ffn_in['sh_up_w'], 'L0_ffn_sh_down_w': _L0_ffn_in['sh_down_w']}

def reference(x, ctx_1024, L0_attn_w_qkv, L0_attn_ln_w, L0_attn_w_proj, L0_xattn_ln_gamma, L0_xattn_ln_beta, L0_xattn_w_q, L0_xattn_w_kv, L0_xattn_w_out, L0_xattn_b_out, L0_xattn_gate, L0_ffn_router_w, L0_ffn_bias, L0_ffn_gate_w, L0_ffn_up_w, L0_ffn_down_w, L0_ffn_sh_gate_w, L0_ffn_sh_up_w, L0_ffn_sh_down_w):
    import jax
    import jax.numpy as jnp

    def _L0_attn_ref(x, w_qkv, ln_w, w_proj):
        import jax, jax.numpy as jnp
        import numpy as np
        B, T, C = (4, 512, 128)
        H = 16
        LS = 32
        EPS = 1e-06

        def rmsnorm(x, w):
            xf = x.astype(jnp.float32)
            y = xf * jax.lax.rsqrt(jnp.mean(xf * xf, axis=-1, keepdims=True) + EPS)
            return y.astype(x.dtype) * w
        Bx, Tx, Cx = x.shape
        ng = Tx // LS
        hd = Cx // H
        xg = x.reshape(Bx, ng, LS, Cx)
        qkv = jnp.einsum('bglc,cd->bgld', xg, w_qkv)
        q, k, v = jnp.split(qkv, 3, axis=-1)
        q = rmsnorm(q, ln_w)
        k = rmsnorm(k, ln_w)
        q = q.reshape(Bx, ng, LS, H, hd).transpose(0, 1, 3, 2, 4)
        k = k.reshape(Bx, ng, LS, H, hd).transpose(0, 1, 3, 2, 4)
        v = v.reshape(Bx, ng, LS, H, hd).transpose(0, 1, 3, 2, 4)
        scale = 1.0 / np.sqrt(hd)
        att = jnp.einsum('bghqd,bghkd->bghqk', q, k) * scale
        causal = jnp.tril(jnp.ones((LS, LS), dtype=bool))
        att = jnp.where(causal, att, -jnp.finfo(att.dtype).max)
        att = jax.nn.softmax(att, axis=-1)
        y = jnp.einsum('bghqk,bghkd->bghqd', att, v)
        y = y.transpose(0, 1, 3, 2, 4).reshape(Bx, Tx, Cx)
        return jnp.einsum('btc,cd->btd', y, w_proj)

    def _L0_xattn_ref(x, context, ln_gamma, ln_beta, w_q, w_kv, w_out, b_out, gate):
        import jax, jax.numpy as jnp
        import numpy as np
        DIM = 128
        NUM_HEADS = 16
        DIM_HEAD = 64
        INNER = NUM_HEADS * DIM_HEAD
        SCALE = DIM_HEAD ** (-0.5)

        def _layernorm(x, gamma, beta, eps=1e-05):
            mu = jnp.mean(x, axis=-1, keepdims=True)
            var = jnp.mean(jnp.square(x - mu), axis=-1, keepdims=True)
            return (x - mu) * jax.lax.rsqrt(var + eps) * gamma + beta
        B, SQ, _ = x.shape
        SK = context.shape[1]
        xn = _layernorm(x, ln_gamma, ln_beta)
        q = (xn @ w_q).reshape(B, SQ, NUM_HEADS, DIM_HEAD)
        kv = context @ w_kv
        k, v = jnp.split(kv, 2, axis=-1)
        k = k.reshape(B, SK, NUM_HEADS, DIM_HEAD)
        v = v.reshape(B, SK, NUM_HEADS, DIM_HEAD)
        scores = jnp.einsum('bqhd,bkhd->bhqk', q * SCALE, k)
        attn = jax.nn.softmax(scores, axis=-1)
        out = jnp.einsum('bhqk,bkhd->bqhd', attn, v).reshape(B, SQ, INNER)
        out = out @ w_out + b_out
        return out * jnp.tanh(gate[0])

    def _L0_ffn_ref(hidden_states, router_w, bias, gate_w, up_w, down_w, sh_gate_w, sh_up_w, sh_down_w):
        import jax, jax.numpy as jnp
        import numpy as np
        B, S, D = (1, 256, 128)
        E, F = (16, 128)
        NG, TKG, K = (4, 2, 4)
        NSH = 2
        SCALE = 2.5
        STD = 0.02
        EPG = E // NG

        def _route(x_flat, router_w, bias):
            logits = x_flat.astype(jnp.float32) @ router_w.T
            scores = jax.nn.sigmoid(logits)
            s = scores + bias[None, :]
            sg = s.reshape(-1, NG, EPG)
            group_score = jax.lax.top_k(sg, 2)[0].sum(-1)
            gidx = jax.lax.top_k(group_score, TKG)[1]
            gmask = jnp.sum(jax.nn.one_hot(gidx, NG, dtype=jnp.float32), axis=1) > 0
            emask = jnp.repeat(gmask, EPG, axis=1)
            masked = jnp.where(emask, s, -1.0)
            topk_idx = jax.lax.top_k(masked, K)[1]
            tw = jnp.take_along_axis(scores, topk_idx, axis=1)
            tw = tw / (tw.sum(-1, keepdims=True) + 1e-20)
            tw = tw * SCALE
            return (topk_idx, tw)
        x = hidden_states.reshape(-1, D)
        topk_idx, tw = _route(x, router_w, bias)
        combine = (jax.nn.one_hot(topk_idx, E, dtype=tw.dtype) * tw[..., None]).sum(1)
        h = jnp.einsum('td,edf->etf', x, gate_w)
        u = jnp.einsum('td,edf->etf', x, up_w)
        y = jnp.einsum('etf,efd->etd', jax.nn.silu(h) * u, down_w)
        routed = jnp.einsum('etd,te->td', y, combine)
        sh = jax.nn.silu(x @ sh_gate_w) * (x @ sh_up_w) @ sh_down_w
        return (routed + sh).reshape(hidden_states.shape)
    x = x + _L0_attn_ref(_layernorm(x, axis=-1), L0_attn_w_qkv, L0_attn_ln_w, L0_attn_w_proj)
    x = x + _L0_xattn_ref(_layernorm(x, axis=-1), ctx_1024, L0_xattn_ln_gamma, L0_xattn_ln_beta, L0_xattn_w_q, L0_xattn_w_kv, L0_xattn_w_out, L0_xattn_b_out, L0_xattn_gate)
    x = x + _L0_ffn_ref(_layernorm(x, axis=-1), L0_ffn_router_w, L0_ffn_bias, L0_ffn_gate_w, L0_ffn_up_w, L0_ffn_down_w, L0_ffn_sh_gate_w, L0_ffn_sh_up_w, L0_ffn_sh_down_w)
    return x

_drawn_inputs = setup_inputs


def setup_inputs(seed=0):
    import zlib

    import numpy as np

    out = dict(_drawn_inputs(seed))
    spreads = {'L0_attn_ln_w': (1.0, 0.2),
     'L0_xattn_ln_gamma': (1.0, 0.6),
     'L0_xattn_ln_beta': (0.0, 0.747),
     'L0_xattn_b_out': (0.0, 0.1),
     'L0_ffn_bias': (0.0, 0.8)}
    factors = {'L0_ffn_router_w': 8.0,
     'L0_ffn_gate_w': 8.0,
     'L0_ffn_up_w': 8.0,
     'L0_ffn_down_w': 8.0,
     'L0_ffn_sh_gate_w': 7.826,
     'L0_ffn_sh_up_w': 7.737,
     'L0_ffn_sh_down_w': 7.755}
    for name, (base, spread) in spreads.items():
        noise = np.random.default_rng([zlib.crc32(name.encode()), seed]).standard_normal(out[name].shape)
        drawn = base * np.exp(spread * noise) if base else spread * noise
        out[name] = jnp.asarray(drawn.astype(out[name].dtype))
    for name, factor in factors.items():
        out[name] = (out[name] * factor).astype(out[name].dtype)
    return out
```

```python
from contextlib import ExitStack

import concourse.bass as bass
from concourse import mybir

F32 = mybir.dt.float32
F32R = mybir.dt.float32r
ALU = mybir.AluOpType
ACT = mybir.ActivationFunctionType
AX = mybir.AxisListType

P = 128
QUAD = 32


def decoder_layer(
    nc: bass.Bass,
    x_in: bass.AP,
    ctx_in: bass.AP,
    w_qkv: bass.AP,
    ln_w: bass.AP,
    w_proj: bass.AP,
    gamma: bass.AP,
    beta: bass.AP,
    w_q: bass.AP,
    w_kv: bass.AP,
    w_out: bass.AP,
    b_out: bass.AP,
    gate: bass.AP,
    router_w: bass.AP,
    router_bias: bass.AP,
    gate_w: bass.AP,
    up_w: bass.AP,
    down_w: bass.AP,
    sh_gate_w: bass.AP,
    sh_up_w: bass.AP,
    sh_down_w: bass.AP,
    out: bass.AP,
):
    B, T, D = x_in.shape
    NT = B * T // P
    TPB = T // P
    LS = 32
    HD = 8
    H1 = D // HD
    NR = 4
    NG = P // LS
    HR = H1 // NR
    VA = HR * (HD + 1)
    CTX = ctx_in.shape[1]
    INNER = w_q.shape[1]
    DH = 64
    H2 = INNER // DH
    NPAIR = H2 // 2
    E, _, F = gate_w.shape
    NSH = sh_gate_w.shape[1] // F
    NE = E + NSH
    NGRP = 4
    EPG = E // NGRP
    TOPK = 4
    CHUNK = 512
    NCH = B * T // CHUNK
    TPC = CHUNK // P
    LN_EPS = 1e-5
    RMS_EPS = 1e-6
    NEG = -3.0e38
    assert D == P and F == P and CTX == 64 and HR == 4 and NR * QUAD == P and LS == QUAD

    with ExitStack() as ctx:
        def sb(name, shape, dt=F32):
            return ctx.enter_context(nc.sbuf_tensor(name, shape, dt))

        def sem(name):
            return ctx.enter_context(nc.semaphore(name))

        bank = [ctx.enter_context(nc.psum_tensor(f"bank{i}", [P, 512], F32)) for i in range(4, 8)]
        wide = ctx.enter_context(nc.psum_tensor("wide", [P, 4, 512], F32))
        bank = [wide[:, i, :] for i in range(4)] + [b[:, :] for b in bank]

        wqkv_sb = sb("wqkv_sb", [P, 3 * D])
        wproj_sb = sb("wproj_sb", [P, D])
        wq_sb = sb("wq_sb", [P, INNER])
        wkv_sb = sb("wkv_sb", [P, 2 * INNER])
        wout_sb = sb("wout_sb", [P, NPAIR, D])
        lnw_col = sb("lnw_col", [P, 1])
        gamma_col = sb("gamma_col", [P, 1])
        beta_col = sb("beta_col", [P, 1])
        row = sb("row", [1, D + E + 1])
        rowb = sb("rowb", [P, D + E + 1])
        rw_sb = sb("rw_sb", [E, D])
        rwT = sb("rwT", [P, E])
        ctx_sb = sb("ctx_sb", [P, 2, D])
        gu_w = sb("gu_w", [P, 2, NE, F])
        gu_hi = sb("gu_hi", [P, 2, NE, F], F32R)
        gu_lo = sb("gu_lo", [P, 2, NE, F], F32R)
        dn_w = sb("dn_w", [P, NE, D])
        ident = sb("ident", [P, P])
        causal = sb("causal", [P, LS])
        headsel = sb("headsel", [P, H1])
        hmask = sb("hmask", [P, HR])
        wq_col = sb("wq_col", [P, 1])
        half = sb("half", [P, 2])
        tgate = sb("tgate", [P, 1])
        bias_out = sb("bias_out", [P, D])
        x = sb("x", [P, NT, D])
        stats = sb("stats", [P, 3, 2, 6])
        mv = sb("mv", [P, 3, NT, 2])
        ve = sb("ve", [P, 3, NT, 1])
        rstd = sb("rstd", [P, 3, NT, 1])
        xn = sb("xn", [P, 3, 2, D])
        xnT = sb("xnT", [P, 2, P])
        sq = sb("sq", [P, 2, D])
        ss = sb("ss", [P, NT, 2])
        ms = sb("ms", [P, NT, 2])
        rqk = sb("rqk", [P, NT, 2])
        qkn = sb("qkn", [P, 2, 2, D])
        qT = sb("qT", [P, 2, P])
        kbd = sb("kbd", [P, 2, NG, HR, LS])
        vbd = sb("vbd", [P, 3, NG, NR, HR, HD + 1])
        s1 = sb("s1", [P, 2, H1, LS])
        mx1 = sb("mx1", [P, 2, H1])
        p1 = sb("p1", [P, 2, H1 * LS])
        p1T = sb("p1T", [P, NR, P])
        rs1 = sb("rs1", [P, H1])
        yn = sb("yn", [P, H1, HD])
        yT = sb("yT", [P, P])
        ctxT = sb("ctxT", [P, B, CTX])
        wqT = sb("wqT", [P, NPAIR, D])
        k2 = sb("k2", [P, 2, B, 2, CTX])
        v2 = sb("v2", [P, 2, B, 2, CTX])
        qk_fold = sb("qk_fold", [P, B, NPAIR, 2 * CTX])
        vo_fold = sb("vo_fold", [P, NPAIR, B, D])
        xn2T = sb("xn2T", [P, 2, P])
        s2 = sb("s2", [P, 2, H2, CTX])
        mx2 = sb("mx2", [P, 2, H2])
        p2 = sb("p2", [P, 2, H2, CTX])
        sum2 = sb("sum2", [P, 2, H2])
        rs2 = sb("rs2", [P, 2, H2])
        p2T = sb("p2T", [P, NPAIR, P])
        xb = sb("xb", [P, 2, D])
        x3T = sb("x3T", [P, 2, P])
        x3hi = sb("x3hi", [P, NT * P], F32R)
        x3lo = sb("x3lo", [P, NT * P], F32R)
        eneg = sb("eneg", [P, NT, E])
        score = sb("score", [P, NT, E])
        biased = sb("biased", [P, NT, E])
        r_a = sb("r_a", [P, NT, E])
        r_b = sb("r_b", [P, NT, E])
        r_c = sb("r_c", [P, NT, E])
        r_p = sb("r_p", [P, NT, NGRP, 2])
        r_q = sb("r_q", [P, NT, NGRP, 2])
        r_g = sb("r_g", [P, 6, NT, NGRP])
        cmp_a = sb("cmp_a", [P, NT, NGRP, NGRP])
        cmp_b = sb("cmp_b", [P, NT, NGRP, NGRP])
        lower = sb("lower", [P, NGRP, NGRP])
        top8 = sb("top8", [P, NT, 8])
        need = sb("need", [P, NT])
        wsum = sb("wsum", [P, NT])
        combine = sb("combine", [P, NT, E])
        ones_col = sb("ones_col", [P, 1])
        sil = p2[:, :, :, :].rearrange("p b h k -> p (b h k)")[:, 0:2 * CHUNK].rearrange("p (b n) -> p b n", b=2)
        act = s2[:, :, :, :].rearrange("p b h k -> p (b h k)")[:, 0:3 * CHUNK].rearrange("p (b n) -> p b n", b=3)

        x_in_s = [sem(f"x_loaded{i}") for i in range(NT)]
        wqkv_l = sem("wqkv_loaded")
        small_l = sem("small_loaded")
        row_l = sem("row_loaded")
        rw_l = sem("router_loaded")
        ctx_l = sem("ctx_loaded")
        wq_l = sem("wq_loaded")
        wkv_l = sem("wkv_loaded")
        wout_l = sem("wout_loaded")
        wproj_l = sem("wproj_loaded")
        gu_l = [sem(f"gu_loaded{i}") for i in range(3)]
        dn_l = sem("dn_loaded")
        stored = sem("stored")
        zeroed = sem("zeroed")
        ident_r = sem("ident_ready")
        const_r = sem("const_ready")
        headsel_r = sem("headsel_ready")
        hm_r = sem("hmask_ready")
        rowb_r = sem("rowb_ready")
        tg_r = sem("tgate_ready")
        bo_r = sem("bias_out_ready")
        bn_s = [sem(f"bn{i}") for i in range(3)]
        mv_s = [sem(f"mv{i}") for i in range(3)]
        ve_s = [sem(f"ve{i}") for i in range(3)]
        rstd_s = [sem(f"rstd{i}") for i in range(3)]
        xn_s = [sem(f"xn{i}") for i in range(3)]
        xT_s = [sem(f"xT{i}") for i in range(3)]
        xnT_s = sem("xnT_copied")
        qk_s = sem("qk_done")
        v_s = sem("v_done")
        ss_s = sem("squares_summed")
        ms_s = sem("mean_squares")
        rqk_s = sem("rqk")
        qkn_s = sem("qk_normed")
        vbd_s = sem("vbd_copied")
        qTp_s = sem("q_transposed")
        kTp_s = sem("k_transposed")
        qT_s = sem("qT_copied")
        kbd_s = sem("kbd_built")
        S1_s = sem("scores1")
        sm1_s = sem("masked1")
        mx1_s = sem("max1")
        sub1_s = sem("sub1")
        p1_s = sem("exp1")
        p1T_s = sem("p1_transposed")
        p1Tc_s = sem("p1T_copied")
        y1_s = sem("pv1")
        rs1_s = sem("rs1")
        yn_s = sem("y_normed")
        yTp_s = sem("y_transposed")
        yT_s = sem("yT_copied")
        o1_s = sem("proj_done")
        res1_s = sem("residual1")
        f_ready = sem("fold_ready")
        f_copied = sem("fold_copied")
        xn2T_s = sem("xn2T_copied")
        S2_s = sem("scores2")
        mx2_s = sem("max2")
        sub2_s = sem("sub2")
        p2_s = sem("exp2")
        sum2_s = sem("sum2")
        rs2_s = sem("rs2")
        pn2_s = sem("p2_normed")
        p2T_s = sem("p2_transposed")
        p2Tc_s = sem("p2T_copied")
        o2_s = sem("out2")
        xb_s = sem("xb")
        res2_s = sem("residual2")
        wsplit_hi = sem("w_hi")
        wsplit_lo = sem("w_lo")
        x3T_s = sem("x3T_copied")
        x3hi_s = sem("x3hi")
        x3lo_s = sem("x3lo")
        rwT_p = sem("rw_transposed")
        rwT_s = sem("rwT_copied")
        lg_s = sem("logits")
        eneg_s = sem("exp_logits")
        route = sem("route_step")
        comb_s = sem("combine_ready")
        h_s = sem("h_done")
        u_s = sem("u_done")
        sil_s = sem("silu_done")
        g_s = sem("act_done")
        y_s = sem("down_done")
        acc_s = sem("accumulated")

        T1, QK, FOLD, PV = bank[4], bank[5], bank[6], bank[7]
        VCOL, KCOL = 2 * P, 2 * D
        OUT2 = bank[5]
        PT2 = [bank[6], bank[7]]

        order = list(range(E, NE)) + list(range(E))
        chunks = [(e, c) for e in order for c in range(NCH)]
        NK = len(chunks)

        units = [("ctx", 0), ("wq", 0), ("wq", 1)]
        for j in range(NPAIR):
            units += [("kv", j), ("A", j), ("VW", j)]
        unit_no = {u: n for n, u in enumerate(units)}
        SKEW = 2
        STEPS = NT + SKEW
        per_step = -(-len(units) // NT)

        def units_of(i):
            return units[i * per_step:(i + 1) * per_step] if i < NT else []

        block = ctx.enter_context(nc.Block())

        @block.sync
        def _(sp):
            xt = x_in.rearrange("b (n p) d -> (b n) p d", p=P)
            sp.dma_start(x[:, 0, :], xt[0]).then_inc(x_in_s[0], 16)
            sp.dma_start(wqkv_sb[:, :], w_qkv).then_inc(wqkv_l, 16)
            sp.dma_start(x[:, 1, :], xt[1]).then_inc(x_in_s[1], 16)
            sp.dma_start(ctx_sb[:, :, :], ctx_in.rearrange("(n c) s d -> (c s) n d", c=2)).then_inc(ctx_l, 16)
            sp.dma_start(lnw_col[:, :], ln_w.rearrange("(p o) -> p o", o=1)).then_inc(small_l, 16)
            sp.dma_start(gamma_col[:, :], gamma.rearrange("(p o) -> p o", o=1)).then_inc(small_l, 16)
            sp.dma_start(beta_col[:, :], beta.rearrange("(p o) -> p o", o=1)).then_inc(small_l, 16)
            sp.dma_start(row[:, 0:D], b_out.rearrange("(o d) -> o d", o=1)).then_inc(row_l, 16)
            sp.dma_start(row[:, D:D + E], router_bias.rearrange("(o d) -> o d", o=1)).then_inc(row_l, 16)
            sp.dma_start(row[:, D + E:D + E + 1], gate.rearrange("(o d) -> o d", o=1)).then_inc(row_l, 16)
            sp.dma_start(wq_sb[:, :], w_q).then_inc(wq_l, 16)
            sp.dma_start(wkv_sb[:, :], w_kv).then_inc(wkv_l, 16)
            sp.dma_start(wproj_sb[:, :], w_proj).then_inc(wproj_l, 16)
            sp.dma_start(wout_sb[:, :, :], w_out.rearrange("(j p) d -> p j d", p=P)).then_inc(wout_l, 16)
            for t in range(2, NT):
                sp.dma_start(x[:, t, :], xt[t]).then_inc(x_in_s[t], 16)
            sp.dma_start(rw_sb[:, :], router_w).then_inc(rw_l, 16)
            sp.dma_start(gu_w[:, 0, E:NE, :], sh_gate_w.rearrange("d (e f) -> d e f", f=F)).then_inc(gu_l[0], 16)
            sp.dma_start(gu_w[:, 1, E:NE, :], sh_up_w.rearrange("d (e f) -> d e f", f=F)).then_inc(gu_l[0], 16)
            for n in range(2):
                es = slice(n * E // 2, (n + 1) * E // 2)
                sp.dma_start(gu_w[:, 0, es, :], gate_w[es].rearrange("e d f -> d e f")).then_inc(gu_l[n + 1], 16)
                sp.dma_start(gu_w[:, 1, es, :], up_w[es].rearrange("e d f -> d e f")).then_inc(gu_l[n + 1], 16)
            sp.dma_start(dn_w[:, E:NE, :], sh_down_w.rearrange("(e f) d -> f e d", f=F)).then_inc(dn_l, 16)
            sp.dma_start(dn_w[:, 0:E, :], down_w.rearrange("e f d -> f e d")).then_inc(dn_l, 16)
            ot = out.rearrange("b (n p) d -> (b n) p d", p=P)
            for t in range(NT):
                sp.wait_ge(acc_s, NT * (NE - 1) + t + 1)
                sp.dma_start(ot[t], x[:, t, :]).then_inc(stored, 16)
            sp.wait_ge(stored, 16 * NT)

        @block.gpsimd
        def _(pool):
            pool.memset(ident[:, :], 0.0).then_inc(zeroed, 1)
            pool.memset(half[:, :], -0.5).then_inc(zeroed, 1)
            pool.memset(causal[:, :], 0.0).then_inc(zeroed, 1)
            pool.memset(headsel[:, :], 1.0).then_inc(zeroed, 1)
            pool.memset(lower[:, :, :], 1.0).then_inc(zeroed, 1)
            pool.memset(vbd[:, :, :, :, :, :], 0.0).then_inc(zeroed, 1)
            pool.memset(k2[:, :, :, :, :], 0.0).then_inc(zeroed, 1)
            pool.memset(v2[:, :, :, :, :], 0.0).then_inc(zeroed, 1)
            pool.memset(ones_col[:, :], 1.0).then_inc(zeroed, 1)
            pool.wait_ge(zeroed, 9)
            pool.affine_select(out=ident[:, :], in_=ident[:, :], compare_op=ALU.not_equal, fill=1.0, base=0,
                               pattern=[[-1, P]], channel_multiplier=1).then_inc(ident_r, 1)
            pool.wait_ge(ident_r, 1)
            for g in range(NG):
                q = causal[QUAD * g:QUAD * (g + 1), :]
                pool.affine_select(out=q, in_=q, compare_op=ALU.is_ge, fill=NEG, base=0,
                                   pattern=[[-1, LS]], channel_multiplier=1).then_inc(const_r, 1)
                pool.wait_ge(const_r, g + 1)
            for h in range(HR):
                pool.memset(vbd[QUAD * h:QUAD * (h + 1), :, :, :, h, HD:HD + 1], 1.0).then_inc(const_r, 1)
                pool.wait_ge(const_r, NG + h + 1)
            pool.affine_select(out=lower[:, :, :], in_=lower[:, :, :], compare_op=ALU.is_gt, fill=0.0, base=0,
                               pattern=[[1, NGRP], [-1, NGRP]], channel_multiplier=0).then_inc(const_r, 1)
            pool.affine_select(out=headsel[:, :], in_=headsel[:, :], compare_op=ALU.is_ge, fill=0.0, base=0,
                               pattern=[[-HD, H1]], channel_multiplier=1).then_inc(headsel_r, 1)
            pool.wait_ge(headsel_r, 1)
            pool.affine_select(out=headsel[:, :], in_=headsel[:, :], compare_op=ALU.is_ge, fill=0.0, base=HD - 1,
                               pattern=[[HD, H1]], channel_multiplier=-1).then_inc(headsel_r, 1)
            pool.wait_ge(row_l, 48)
            pool.partition_broadcast(rowb[:, :], row[:, :], P).then_inc(rowb_r, 1)

            def rsqrt_var(n, t, scale, eps):
                pool.wait_ge(mv_s[n], t + 1)
                pool.tensor_scalar(ve[:, n, t, :], mv[:, n, t, 1:2], scale, eps, ALU.mult, ALU.add).then_inc(ve_s[n], 1)
                pool.wait_ge(ve_s[n], t + 1)
                pool.tensor_tensor(rstd[:, n, t, :], ve[:, n, t, :], half[:, 0:1], ALU.pow).then_inc(rstd_s[n], 1)

            def rms(t):
                pool.wait_ge(ss_s, 2 * (t + 1))
                pool.tensor_scalar(ms[:, t, :], ss[:, t, :], 1.0 / D, RMS_EPS, ALU.mult, ALU.add).then_inc(ms_s, 1)
                pool.wait_ge(ms_s, t + 1)
                pool.tensor_tensor(rqk[:, t, :], ms[:, t, :], half[:, :], ALU.pow).then_inc(rqk_s, 1)

            split = [0]

            def split_weights(n):
                for e in order[split[0]:split[0] + n]:
                    part = 0 if e >= E else 1 + e // (E // 2)
                    pool.wait_ge(gu_l[part], 32)
                    pool.tensor_copy(gu_hi[:, :, e, :], gu_w[:, :, e, :]).then_inc(wsplit_hi, 1)
                    pool.wait_ge(wsplit_hi, split[0] + 1)
                    pool.tensor_tensor(gu_lo[:, :, e, :], gu_w[:, :, e, :], gu_hi[:, :, e, :].bitcast(F32),
                                       ALU.subtract).then_inc(wsplit_lo, 1)
                    split[0] += 1

            def norm_p2(t):
                pool.wait_ge(rs2_s, t + 1)
                pool.tensor_tensor(p2[:, t % 2, :, :], p2[:, t % 2, :, :],
                                   rs2[:, t % 2, :].unsqueeze(2).to_broadcast([P, H2, CTX]),
                                   ALU.mult).then_inc(pn2_s, 1)

            def add_bias(t):
                pool.wait_ge(res1_s, t + 1)
                if t >= 2:
                    pool.wait_ge(res2_s, t - 1)
                pool.tensor_tensor(xb[:, t % 2, :], x[:, t, :], bias_out[:, :], ALU.add).then_inc(xb_s, 1)

            rsqrt_var(0, 0, 1.0, LN_EPS)
            for i in range(2 * STEPS):
                if i + 1 < NT:
                    rsqrt_var(0, i + 1, 1.0, LN_EPS)
                if i < NT:
                    rms(i)
                    if i == 1:
                        pool.wait_ge(tg_r, 1)
                        pool.tensor_scalar(bias_out[:, :], rowb[:, 0:D], tgate[:, :], None, ALU.mult).then_inc(bo_r, 1)
                        pool.wait_ge(bo_r, 1)
                if 3 <= i < NT + 3:
                    split_weights(2)
                if NT + 3 <= i < 2 * NT + 3:
                    rsqrt_var(2, i - NT - 3, 1.0, LN_EPS)
                if NT <= i < 2 * NT:
                    rsqrt_var(1, i - NT, 1.0 + LN_EPS, LN_EPS * LN_EPS)
                if NT + 1 <= i < 2 * NT + 1:
                    norm_p2(i - NT - 1)
                if NT <= i < 2 * NT:
                    add_bias(i - NT)
            split_weights(NE - split[0])

        @block.scalar
        def _(sc):
            sc.wait_ge(rowb_r, 1)
            sc.activation(tgate[:, :], rowb[:, D + E:D + E + 1], ACT.Tanh).then_inc(tg_r, 1)

            def copy_xnT(t):
                sc.wait_ge(xT_s[0], t + 1)
                if t >= 2:
                    sc.wait_ge(v_s, t - 1)
                sc.copy(xnT[:, t % 2, :], T1[:, 0:P]).then_inc(xnT_s, 1)

            def squares(t):
                sc.wait_ge(qk_s, t + 1)
                for n in range(2):
                    if t >= 1:
                        sc.wait_ge(ss_s, 2 * t)
                    sc.activation(sq[:, n, :], QK[:, n * D:(n + 1) * D], ACT.Square,
                                  accum_out=ss[:, t, n:n + 1]).then_inc(ss_s, 1)

            def scale_qk(t):
                sc.wait_ge(rqk_s, t + 1)
                if t >= 2:
                    sc.wait_ge(qTp_s, t - 1)
                for n in range(2):
                    sc.activation(qkn[:, t % 2, n, :], QK[:, n * D:(n + 1) * D], ACT.Copy,
                                  scale=rqk[:, t, n:n + 1]).then_inc(qkn_s, 1)

            def copy_v(t):
                sc.wait_ge(v_s, t + 1)
                if t == 0:
                    sc.wait_ge(const_r, NG + HR)
                if t >= 3:
                    sc.wait_ge(y1_s, t - 2)
                for h in range(HR):
                    qs = slice(QUAD * h, QUAD * (h + 1))
                    sc.copy(vbd[qs, t % 3, :, :, h, 0:HD],
                            T1[qs, VCOL:VCOL + P].rearrange("p (g r d) -> p g r d", g=NG, r=NR)).then_inc(vbd_s, 1)

            def copy_qT(t):
                sc.wait_ge(qTp_s, t + 1)
                if t == 0:
                    sc.wait_ge(hm_r, 3)
                if t >= 2:
                    sc.wait_ge(S1_s, t - 1)
                sc.activation(qT[:, t % 2, :], T1[:, P:2 * P], ACT.Copy, scale=wq_col[:, :]).then_inc(qT_s, 1)

            def exp1(t):
                sc.wait_ge(sub1_s, t + 1)
                if t >= 2:
                    sc.wait_ge(p1T_s, t - 1)
                sc.activation(p1[:, t % 2, :], s1[:, t % 2, :, :].rearrange("p h k -> p (h k)"), ACT.Exp).then_inc(p1_s, 1)

            def copy_p1T(t):
                sc.wait_ge(p1T_s, t + 1)
                if t >= 1:
                    sc.wait_ge(y1_s, t)
                sc.copy(p1T[:, :, :].rearrange("p r q -> p (r q)"), PV[:, :]).then_inc(p1Tc_s, 1)

            def copy_yT(t):
                sc.wait_ge(yTp_s, t + 1)
                if t >= 1:
                    sc.wait_ge(o1_s, t)
                sc.copy(yT[:, :], PV[:, 2 * P:3 * P]).then_inc(yT_s, 1)

            def copy_fold(u):
                kind, j = u
                n = unit_no[u]
                sc.wait_ge(f_ready, n + 1)
                if kind == "ctx":
                    sc.copy(ctxT[:, :, :].rearrange("p b s -> p (b s)"), FOLD[:, 0:B * CTX]).then_inc(f_copied, 1)
                elif kind == "wq":
                    sc.activation(wqT[:, 4 * j:4 * j + 4, :].rearrange("p j d -> p (j d)"), FOLD[:, :], ACT.Copy,
                                  scale=float(DH) ** -0.5).then_inc(f_copied, 1)
                elif kind == "kv":
                    if j == 0:
                        sc.wait_ge(zeroed, 9)
                    for m, dst in enumerate((k2, v2)):
                        for h in range(2):
                            hs = slice(DH * h, DH * (h + 1))
                            last = sc.copy(dst[hs, j % 2, :, h, :],
                                           FOLD[hs, m * B * CTX:(m + 1) * B * CTX].rearrange("p (b s) -> p b s", b=B))
                    last.then_inc(f_copied, 1)
                elif kind == "A":
                    sc.copy(qk_fold[:, :, j, :], FOLD[:, :].rearrange("p (b s) -> p b s", b=B)).then_inc(f_copied, 1)
                else:
                    sc.activation(vo_fold[:, j, :, :].rearrange("p b d -> p (b d)"), FOLD[:, :], ACT.Copy,
                                  scale=tgate[:, :]).then_inc(f_copied, 1)

            def copy_xn2T(t):
                sc.wait_ge(xT_s[1], t + 1)
                if t == 0:
                    sc.wait_ge(small_l, 48)
                if t >= 2:
                    sc.wait_ge(S2_s, t - 1)
                sc.activation(xn2T[:, t % 2, :], T1[:, 0:P], ACT.Identity, scale=gamma_col[:, :],
                              bias=beta_col[:, :]).then_inc(xn2T_s, 1)

            def exp2(t):
                sc.wait_ge(sub2_s, t + 1)
                if t >= 2:
                    sc.wait_ge(p2T_s, t - 1)
                sc.activation(p2[:, t % 2, :, :].rearrange("p h k -> p (h k)"),
                              s2[:, t % 2, :, :].rearrange("p h k -> p (h k)"), ACT.Exp).then_inc(p2_s, 1)

            def copy_p2T(t):
                for n in range(2):
                    sc.wait_ge(p2T_s, t + 1)
                    if t >= 1:
                        sc.wait_ge(o2_s, t)
                    sc.copy(p2T[:, 4 * n:4 * n + 4, :].rearrange("p j q -> p (j q)"), PT2[n]).then_inc(p2Tc_s, 1)

            def copy_x3T(t):
                sc.wait_ge(xT_s[2], t + 1)
                if t >= 2:
                    sc.wait_ge(x3lo_s, t - 1)
                    sc.wait_ge(lg_s, t - 1)
                sc.copy(x3T[:, t % 2, :], T1[:, P:2 * P]).then_inc(x3T_s, 1)
                sc.wait_ge(x3T_s, t + 1)
                sc.copy(x3hi[:, t * P:(t + 1) * P], x3T[:, t % 2, :]).then_inc(x3hi_s, 1)

            def exp_logits(t):
                sc.wait_ge(lg_s, t + 1)
                sc.activation(eneg[:, t, :], T1[:, 2 * P:2 * P + E], ACT.Exp, scale=-1.0).then_inc(eneg_s, 1)

            for i in range(2 * STEPS):
                if i < NT:
                    copy_xnT(i)
                if 2 <= i < NT + 2:
                    copy_p1T(i - 2)
                if i < NT:
                    squares(i)
                if 1 <= i < NT + 1:
                    exp1(i - 1)
                for u in units_of(i)[0:1]:
                    copy_fold(u)
                if i < NT:
                    copy_v(i)
                for u in units_of(i)[1:2]:
                    copy_fold(u)
                if i < NT:
                    scale_qk(i)
                if 2 <= i < NT + 2:
                    copy_yT(i - 2)
                for u in units_of(i)[2:]:
                    copy_fold(u)
                if i < NT:
                    copy_qT(i)
                if i == NT:
                    sc.wait_ge(rwT_p, 1)
                    sc.copy(rwT[:, :], T1[:, 3 * P:3 * P + E]).then_inc(rwT_s, 1)
                if NT <= i < 2 * NT:
                    copy_xn2T(i - NT)
                if NT + 2 <= i < 2 * NT + 2:
                    copy_p2T(i - NT - 2)
                if NT + 1 <= i < 2 * NT + 1:
                    exp2(i - NT - 1)
                if NT + 3 <= i < 2 * NT + 3:
                    copy_x3T(i - NT - 3)
                    exp_logits(i - NT - 3)

            for k, (e, c) in enumerate(chunks):
                sc.wait_ge(h_s, k + 1)
                if k >= 2:
                    sc.wait_ge(g_s, k - 1)
                sc.activation(sil[:, k % 2, :], bank[k % 2], ACT.Silu).then_inc(sil_s, 1)

        @block.vector
        def _(dve):
            def norm_stats(n, t):
                dve.bn_stats(stats[:, n, t % 2, :], x[:, t, :]).then_inc(bn_s[n], 1)
                dve.wait_ge(bn_s[n], t + 1)
                dve.bn_aggr(mv[:, n, t, :], stats[:, n, t % 2, :]).then_inc(mv_s[n], 1)

            def norm_apply(n, t):
                dve.wait_ge(rstd_s[n], t + 1)
                if t >= 2:
                    dve.wait_ge(xT_s[n], t - 1)
                dve.tensor_scalar(xn[:, n, t % 2, :], x[:, t, :], mv[:, n, t, 0:1], rstd[:, n, t, :],
                                  ALU.subtract, ALU.mult).then_inc(xn_s[n], 1)

            def build_kbd(t):
                dve.wait_ge(kTp_s, t + 1)
                if t >= 2:
                    dve.wait_ge(S1_s, t - 1)
                dve.tensor_tensor(kbd[:, t % 2, :, :, :],
                                  QK[:, KCOL:KCOL + P].rearrange("p (g k) -> p g k", g=NG).unsqueeze(2)
                                  .to_broadcast([P, NG, HR, LS]),
                                  hmask[:, :].unsqueeze(1).unsqueeze(3).to_broadcast([P, NG, HR, LS]),
                                  ALU.mult).then_inc(kbd_s, 1)

            def softmax1(t):
                s = s1[:, t % 2, :, :]
                dve.wait_ge(S1_s, t + 1)
                if t == 0:
                    dve.wait_ge(const_r, NG)
                if t >= 2:
                    dve.wait_ge(p1_s, t - 1)
                dve.tensor_tensor(s.rearrange("p (r h) k -> p r h k", r=NR),
                                  wide[:, :, 0:P].rearrange("p r (h k) -> p r h k", h=HR),
                                  causal[:, :].unsqueeze(1).unsqueeze(1).to_broadcast([P, NR, HR, LS]),
                                  ALU.add).then_inc(sm1_s, 1)
                dve.wait_ge(sm1_s, t + 1)
                dve.tensor_reduce(mx1[:, t % 2, :], s, AX.X, ALU.max).then_inc(mx1_s, 1)
                dve.wait_ge(mx1_s, t + 1)
                dve.tensor_tensor(s, s, mx1[:, t % 2, :].unsqueeze(2).to_broadcast([P, H1, LS]),
                                  ALU.subtract).then_inc(sub1_s, 1)

            def norm_y(t):
                y = PV[:, 0:NR * VA].rearrange("p (h d) -> p h d", d=HD + 1)
                dve.wait_ge(y1_s, t + 1)
                if t >= 1:
                    dve.wait_ge(yn_s, t)
                dve.reciprocal(rs1[:, :], y[:, :, HD]).then_inc(rs1_s, 1)
                dve.wait_ge(rs1_s, t + 1)
                if t >= 1:
                    dve.wait_ge(yTp_s, t)
                dve.tensor_tensor(yn[:, :, :], y[:, :, 0:HD], rs1[:, :].unsqueeze(2).to_broadcast([P, H1, HD]),
                                  ALU.mult).then_inc(yn_s, 1)

            def residual1(t):
                dve.wait_ge(o1_s, t + 1)
                dve.tensor_tensor(x[:, t, :], PV[:, 3 * P:4 * P], x[:, t, :], ALU.add).then_inc(res1_s, 1)

            def softmax2_max(t):
                s = wide[:, 2 * (t % 2):2 * (t % 2) + 2, :].rearrange("p b (h k) -> p (b h) k", k=CTX)
                dve.wait_ge(S2_s, t + 1)
                if t >= 2:
                    dve.wait_ge(sub2_s, t - 1)
                dve.tensor_reduce(mx2[:, t % 2, :], s, AX.X, ALU.max).then_inc(mx2_s, 1)
                dve.wait_ge(mx2_s, t + 1)
                if t >= 2:
                    dve.wait_ge(p2_s, t - 1)
                dve.tensor_tensor(s2[:, t % 2, :, :], s, mx2[:, t % 2, :].unsqueeze(2).to_broadcast([P, H2, CTX]),
                                  ALU.subtract).then_inc(sub2_s, 1)

            def softmax2_sum(t):
                dve.wait_ge(p2_s, t + 1)
                dve.tensor_reduce(sum2[:, t % 2, :], p2[:, t % 2, :, :], AX.X, ALU.add).then_inc(sum2_s, 1)
                dve.wait_ge(sum2_s, t + 1)
                if t >= 2:
                    dve.wait_ge(pn2_s, t - 1)
                dve.reciprocal(rs2[:, t % 2, :], sum2[:, t % 2, :]).then_inc(rs2_s, 1)

            def residual2(t):
                dve.wait_ge(o2_s, t + 1)
                dve.wait_ge(xb_s, t + 1)
                dve.wait_ge(xn_s[1], t + 1)
                dve.tensor_tensor(x[:, t, :], OUT2[:, 0:D], xb[:, t % 2, :], ALU.add).then_inc(res2_s, 1)

            def split_x3(t):
                dve.wait_ge(x3hi_s, t + 1)
                dve.tensor_tensor(x3lo[:, t * P:(t + 1) * P], x3T[:, t % 2, :],
                                  x3hi[:, t * P:(t + 1) * P].bitcast(F32), ALU.subtract).then_inc(x3lo_s, 1)

            dve.wait_ge(x_in_s[0], 16)
            norm_stats(0, 0)
            for i in range(2 * STEPS):
                if i + 1 < NT:
                    dve.wait_ge(x_in_s[i + 1], 16)
                    norm_stats(0, i + 1)
                if i < NT:
                    norm_apply(0, i)
                if i == 0:
                    dve.wait_ge(headsel_r, 2)
                    dve.tensor_reduce(hmask[:, :], headsel[:, :].rearrange("p (r h) -> p h r", r=NR), AX.X,
                                      ALU.add).then_inc(hm_r, 1)
                    dve.wait_ge(hm_r, 1)
                    dve.wait_ge(small_l, 48)
                    dve.tensor_scalar(hmask[:, :], hmask[:, :], lnw_col[:, :], None, ALU.mult).then_inc(hm_r, 1)
                    dve.tensor_scalar(wq_col[:, :], lnw_col[:, :], float(HD) ** -0.5, None, ALU.mult).then_inc(hm_r, 1)
                    dve.wait_ge(hm_r, 3)
                if NT <= i < 2 * NT:
                    norm_apply(1, i - NT)
                if NT + 3 <= i < 2 * NT + 3:
                    norm_apply(2, i - NT - 3)
                if 1 <= i < NT + 1:
                    softmax1(i - 1)
                if 2 <= i < NT + 2:
                    norm_y(i - 2)
                if i < NT:
                    build_kbd(i)
                if 2 <= i < NT + 2:
                    residual1(i - 2)
                if NT - 1 <= i < 2 * NT - 1:
                    dve.wait_ge(res1_s, i - NT + 2)
                    norm_stats(1, i - NT + 1)
                if NT + 1 <= i < 2 * NT + 1:
                    softmax2_max(i - NT - 1)
                    softmax2_sum(i - NT - 1)
                if NT + 3 <= i < 2 * NT + 3:
                    split_x3(i - NT - 3)
                if NT + 2 <= i < 2 * NT + 2:
                    residual2(i - NT - 2)
                    dve.wait_ge(res2_s, i - NT - 2 + 1)
                    norm_stats(2, i - NT - 2)

            step = [0]

            def then(ins):
                step[0] += 1
                ins.then_inc(route, 1)
                dve.wait_ge(route, step[0])

            def routing():
                ev, gv = [P, NT, E], [P, NT, NGRP]
                dve.wait_ge(eneg_s, NT)
                then(dve.tensor_scalar(r_a[:, :, :], eneg[:, :, :], 1.0, None, ALU.add))
                then(dve.reciprocal(score[:, :, :], r_a[:, :, :]))
                then(dve.tensor_tensor(biased[:, :, :], score[:, :, :],
                                       rowb[:, D:D + E].unsqueeze(1).to_broadcast(ev), ALU.add))
                quad = biased[:, :, :].rearrange("p t (g a b) -> p t g a b", g=NGRP, a=2)
                v_hi = r_p[:, :, :, :]
                v_lo = r_q[:, :, :, :]
                pairs = biased[:, :, :].rearrange("p t (g a b) -> p (t g) a b", g=NGRP, a=2)
                hi3 = r_p[:, :, :, :].rearrange("p t g a -> p (t g) a")
                lo3 = r_q[:, :, :, :].rearrange("p t g a -> p (t g) a")
                then(dve.tensor_tensor(hi3, pairs[:, :, :, 0], pairs[:, :, :, 1], ALU.max))
                then(dve.tensor_tensor(lo3, pairs[:, :, :, 0], pairs[:, :, :, 1], ALU.min))
                gmax, gmin, lmax, gs, rank, gsel = (r_g[:, n, :, :] for n in range(6))
                then(dve.tensor_tensor(gmax, r_p[:, :, :, 0], r_p[:, :, :, 1], ALU.max))
                then(dve.tensor_tensor(gmin, r_p[:, :, :, 0], r_p[:, :, :, 1], ALU.min))
                then(dve.tensor_tensor(lmax, r_q[:, :, :, 0], r_q[:, :, :, 1], ALU.max))
                then(dve.tensor_tensor(lmax, lmax, gmin, ALU.max))
                then(dve.tensor_tensor(gs, gmax, lmax, ALU.add))
                gg = [P, NT, NGRP, NGRP]
                other = gs.unsqueeze(2).to_broadcast(gg)
                own = gs.unsqueeze(3).to_broadcast(gg)
                then(dve.tensor_tensor(cmp_a[:, :, :, :], other, own, ALU.is_equal))
                then(dve.tensor_tensor(cmp_a[:, :, :, :], cmp_a[:, :, :, :],
                                       lower[:, :, :].unsqueeze(1).to_broadcast(gg), ALU.mult))
                then(dve.tensor_tensor(cmp_b[:, :, :, :], other, own, ALU.is_gt))
                then(dve.tensor_tensor(cmp_a[:, :, :, :], cmp_a[:, :, :, :], cmp_b[:, :, :, :], ALU.add))
                then(dve.tensor_reduce(rank, cmp_a[:, :, :, :], AX.X, ALU.add))
                then(dve.tensor_scalar(gsel, rank, 1.5, None, ALU.is_lt))
                gsel_e = gsel.unsqueeze(3).to_broadcast([P, NT, NGRP, EPG])
                by_group = "p t (g a) -> p t g a"
                then(dve.tensor_tensor(r_a[:, :, :].rearrange(by_group, g=NGRP),
                                       biased[:, :, :].rearrange(by_group, g=NGRP), gsel_e, ALU.mult))
                then(dve.tensor_scalar(gsel, gsel, -1.0, None, ALU.add))
                then(dve.tensor_tensor(r_a[:, :, :].rearrange(by_group, g=NGRP),
                                       r_a[:, :, :].rearrange(by_group, g=NGRP), gsel_e, ALU.add))
                for t in range(NT):
                    last = dve.max(top8[:, t, :], r_a[:, t, :])
                then(last)
                least = top8[:, :, TOPK - 1:TOPK].to_broadcast(ev)
                then(dve.tensor_tensor(r_b[:, :, :], r_a[:, :, :], least, ALU.is_gt))
                then(dve.tensor_reduce(need[:, :], r_b[:, :, :], AX.X, ALU.add))
                then(dve.tensor_scalar(need[:, :], need[:, :], -1.0, TOPK + 0.5, ALU.mult, ALU.add))
                then(dve.tensor_tensor(r_a[:, :, :], r_a[:, :, :], least, ALU.is_equal))
                src, dst = r_a, r_c
                then(dve.tensor_copy(biased[:, :, :], r_a[:, :, :]))
                n = 1
                while n < E:
                    dve.tensor_copy(dst[:, :, 0:n], src[:, :, 0:n]).then_inc(route, 1)
                    step[0] += 1
                    then(dve.tensor_tensor(dst[:, :, n:E], src[:, :, n:E], src[:, :, 0:E - n], ALU.add))
                    src, dst = dst, src
                    n *= 2
                then(dve.tensor_tensor(dst[:, :, :], src[:, :, :], need[:, :].unsqueeze(2).to_broadcast(ev), ALU.is_lt))
                then(dve.tensor_tensor(dst[:, :, :], dst[:, :, :], biased[:, :, :], ALU.mult))
                then(dve.tensor_tensor(r_b[:, :, :], r_b[:, :, :], dst[:, :, :], ALU.add))
                then(dve.tensor_tensor(r_b[:, :, :], r_b[:, :, :], score[:, :, :], ALU.mult))
                then(dve.tensor_reduce(wsum[:, :], r_b[:, :, :], AX.X, ALU.add))
                then(dve.tensor_scalar(wsum[:, :], wsum[:, :], 1e-20, None, ALU.add))
                then(dve.reciprocal(wsum[:, :], wsum[:, :]))
                then(dve.tensor_scalar(wsum[:, :], wsum[:, :], 2.5, None, ALU.mult))
                dve.tensor_tensor(combine[:, :, :], r_b[:, :, :], wsum[:, :].unsqueeze(2).to_broadcast(ev),
                                  ALU.mult).then_inc(comb_s, 1)
                dve.wait_ge(comb_s, 1)

            def multiply(k):
                dve.wait_ge(sil_s, k + 1)
                dve.wait_ge(u_s, k + 1)
                if k >= 3:
                    dve.wait_ge(y_s, k - 2)
                dve.tensor_tensor(act[:, k % 3, :], sil[:, k % 2, :], bank[2 + k % 2], ALU.mult).then_inc(g_s, 1)

            def accumulate(k):
                e, c = chunks[k]
                dve.wait_ge(y_s, k + 1)
                if k >= NCH:
                    dve.wait_ge(acc_s, TPC * (k - NCH + 1))
                for n in range(TPC):
                    t = c * TPC + n
                    w = combine[:, t, e:e + 1] if e < E else ones_col[:, :]
                    dve.scalar_tensor_tensor(out=x[:, t, :], in0=bank[4 + k % 2][:, n * D:(n + 1) * D], scalar=w,
                                             in1=x[:, t, :], op0=ALU.mult, op1=ALU.add).then_inc(acc_s, 1)

            routing()
            for k in range(NK + 2):
                if k < NK:
                    multiply(k)
                if k >= 2:
                    accumulate(k - 2)

        @block.tensor
        def _(pe):
            def transpose_xn(n, t, dst):
                pe.wait_ge(xn_s[n], t + 1)
                pe.transpose(dst, xn[:, n, t % 2, :], ident[:, :]).then_inc(xT_s[n], 1)

            def project_qkv(t):
                pe.wait_ge(xnT_s, t + 1)
                if t == 0:
                    pe.wait_ge(wqkv_l, 16)
                if t >= 1:
                    pe.wait_ge(kbd_s, t)
                pe.matmul(QK[:, 0:2 * D], xnT[:, t % 2, :], wqkv_sb[:, 0:2 * D], start=True, stop=True).then_inc(qk_s, 1)

            def project_v(t):
                for h in range(HR):
                    wv = wqkv_sb[:, 2 * D:3 * D].rearrange("p (r h d) -> p r h d", r=NR, h=HR)[:, :, h, :]
                    for g in range(NG):
                        last = pe.matmul(T1[QUAD * h:QUAD * (h + 1), VCOL + QUAD * g:VCOL + QUAD * (g + 1)],
                                         xnT[:, t % 2, LS * g:LS * (g + 1)], wv, start=True, stop=True)
                last.then_inc(v_s, 1)

            def transpose_qk(t):
                pe.wait_ge(qkn_s, 2 * (t + 1))
                pe.transpose(QK[:, KCOL:KCOL + P], qkn[:, t % 2, 1, :], ident[:, :]).then_inc(kTp_s, 1)
                pe.wait_ge(vbd_s, HR * (t + 1))
                pe.transpose(T1[:, P:2 * P], qkn[:, t % 2, 0, :], ident[:, :]).then_inc(qTp_s, 1)

            def scores1(t):
                pe.wait_ge(qT_s, t + 1)
                pe.wait_ge(kbd_s, t + 1)
                if t >= 1:
                    pe.wait_ge(sm1_s, t)
                for g in range(NG):
                    for r in range(NR):
                        rows = slice(QUAD * r, QUAD * (r + 1))
                        last = pe.matmul(wide[QUAD * g:QUAD * (g + 1), r, 0:P], qT[rows, t % 2, LS * g:LS * (g + 1)],
                                         kbd[rows, t % 2, g, :, :].rearrange("p h k -> p (h k)"), start=True, stop=True)
                last.then_inc(S1_s, 1)

            def transpose_p1(t):
                pe.wait_ge(p1_s, t + 1)
                if t >= 1:
                    pe.wait_ge(res1_s, t)
                for r in range(NR):
                    last = pe.transpose(PV[:, r * P:(r + 1) * P], p1[:, t % 2, r * P:(r + 1) * P], ident[:, :])
                last.then_inc(p1T_s, 1)

            def values1(t):
                pe.wait_ge(p1Tc_s, t + 1)
                pe.wait_ge(vbd_s, HR * (t + 1))
                for r in range(NR):
                    for g in range(NG):
                        last = pe.matmul(PV[QUAD * g:QUAD * (g + 1), r * VA:(r + 1) * VA],
                                         p1T[:, r, LS * g:LS * (g + 1)],
                                         vbd[:, t % 3, g, r, :, :].rearrange("p h d -> p (h d)"), start=True, stop=True)
                last.then_inc(y1_s, 1)

            def project_y(t):
                pe.wait_ge(yn_s, t + 1)
                pe.transpose(PV[:, 2 * P:3 * P], yn[:, :, :].rearrange("p h d -> p (h d)"), ident[:, :]).then_inc(yTp_s, 1)

            def project_out(t):
                if t == 0:
                    pe.wait_ge(wproj_l, 16)
                pe.wait_ge(yT_s, t + 1)
                pe.matmul(PV[:, 3 * P:4 * P], yT[:, :], wproj_sb[:, :], start=True, stop=True).then_inc(o1_s, 1)

            def fold(u):
                kind, j = u
                n = unit_no[u]
                if n >= 1:
                    pe.wait_ge(f_copied, n)
                if kind == "ctx":
                    pe.wait_ge(ctx_l, 16)
                    for m in range(2):
                        last = pe.transpose(FOLD[:, m * P:(m + 1) * P], ctx_sb[:, m, :], ident[:, :])
                elif kind == "wq":
                    pe.wait_ge(wq_l, 16)
                    for m in range(4):
                        last = pe.transpose(FOLD[:, m * P:(m + 1) * P], wq_sb[:, (4 * j + m) * P:(4 * j + m + 1) * P],
                                            ident[:, :])
                elif kind == "kv":
                    pe.wait_ge(wkv_l, 16)
                    for m in range(2):
                        last = pe.matmul(FOLD[:, m * B * CTX:(m + 1) * B * CTX],
                                         wkv_sb[:, m * INNER + j * P:m * INNER + (j + 1) * P],
                                         ctxT[:, :, :].rearrange("p b s -> p (b s)"), start=True, stop=True)
                elif kind == "A":
                    last = pe.matmul(FOLD[:, :], wqT[:, j, :], k2[:, j % 2, :, :, :].rearrange("p b h s -> p (b h s)"),
                                     start=True, stop=True)
                else:
                    pe.wait_ge(wout_l, 16)
                    for b in range(B):
                        last = pe.matmul(FOLD[:, b * D:(b + 1) * D], v2[:, j % 2, b, :, :].rearrange("p h s -> p (h s)"),
                                         wout_sb[:, j, :], start=True, stop=True)
                last.then_inc(f_ready, 1)

            def scores2(t):
                b = t // TPB
                pe.wait_ge(xn2T_s, t + 1)
                if t == 0:
                    pe.wait_ge(sm1_s, NT)
                    pe.wait_ge(f_copied, len(units))
                if t >= 2:
                    pe.wait_ge(sub2_s, t - 1)
                fold_b = qk_fold[:, b, :, :].rearrange("p j s -> p (j s)")
                for n in range(2):
                    last = pe.matmul(wide[:, 2 * (t % 2) + n, :], xn2T[:, t % 2, :], fold_b[:, n * 512:(n + 1) * 512],
                                     start=True, stop=True)
                last.then_inc(S2_s, 1)

            def transpose_p2(t):
                pe.wait_ge(pn2_s, t + 1)
                if t == 0:
                    pe.wait_ge(res1_s, NT)
                if t >= 1:
                    pe.wait_ge(p2Tc_s, 2 * t)
                for j in range(NPAIR):
                    last = pe.transpose(PT2[j // 4][:, (j % 4) * P:(j % 4 + 1) * P], p2[:, t % 2, 2 * j:2 * j + 2, :].rearrange("p h k -> p (h k)"),
                                        ident[:, :])
                last.then_inc(p2T_s, 1)

            def output2(t):
                b = t // TPB
                pe.wait_ge(p2Tc_s, 2 * (t + 1))
                if t >= 1:
                    pe.wait_ge(res2_s, t)
                for j in range(NPAIR):
                    last = pe.matmul(OUT2[:, 0:D], p2T[:, j, :], vo_fold[:, j, b, :], start=(j == 0), stop=(j == NPAIR - 1))
                last.then_inc(o2_s, 1)

            def logits(t):
                pe.wait_ge(x3T_s, t + 1)
                pe.matmul(T1[:, 2 * P:2 * P + E], x3T[:, t % 2, :], rwT[:, :], start=True, stop=True).then_inc(lg_s, 1)

            pe.wait_ge(ident_r, 1)
            for i in range(2 * STEPS):
                us = units_of(i)
                if i < NT:
                    if i >= 1:
                        pe.wait_ge(qT_s, i)
                    transpose_xn(0, i, T1[:, 0:P])
                if 2 <= i < NT + 2:
                    transpose_p1(i - 2)
                if i < NT:
                    project_qkv(i)
                    project_v(i)
                for u in us[0:1]:
                    fold(u)
                if 1 <= i < NT + 1:
                    scores1(i - 1)
                if 2 <= i < NT + 2:
                    values1(i - 2)
                for u in us[1:2]:
                    fold(u)
                if i < NT:
                    transpose_qk(i)
                if 2 <= i < NT + 2:
                    project_y(i - 2)
                for u in us[2:]:
                    fold(u)
                if 2 <= i < NT + 2:
                    project_out(i - 2)
                if i == NT:
                    pe.wait_ge(qT_s, NT)
                    pe.wait_ge(rw_l, 16)
                    pe.transpose(T1[:, 3 * P:3 * P + E], rw_sb[:, :], ident[0:E, 0:E]).then_inc(rwT_p, 1)
                    pe.wait_ge(rwT_s, 1)
                if NT <= i < 2 * NT:
                    if i - NT - 4 >= 0:
                        pe.wait_ge(eneg_s, i - NT - 4 + 1)
                    if i > NT:
                        pe.wait_ge(xn2T_s, i - NT)
                    transpose_xn(1, i - NT, T1[:, 0:P])
                if NT + 2 <= i < 2 * NT + 2:
                    transpose_p2(i - NT - 2)
                if NT <= i < 2 * NT:
                    scores2(i - NT)
                if NT + 2 <= i < 2 * NT + 2:
                    output2(i - NT - 2)
                if NT + 3 <= i < 2 * NT + 3:
                    t = i - NT - 3
                    pe.wait_ge(xn2T_s, min(i - NT + 1, NT))
                    if t >= 1:
                        pe.wait_ge(eneg_s, t)
                    transpose_xn(2, t, T1[:, P:2 * P])
                    logits(t)

            def gate_up(k):
                e, c = chunks[k]
                pe.wait_ge(wsplit_lo, order.index(e) + 1)
                pe.wait_ge(wsplit_hi, order.index(e) + 1)
                pe.wait_ge(x3lo_s, TPC * (c + 1))
                if k == 0:
                    pe.wait_ge(sub2_s, NT)
                if k >= 2:
                    pe.wait_ge(g_s, k - 1)
                cols = slice(c * CHUNK, (c + 1) * CHUNK)
                for m, (dst, done) in enumerate(((bank[k % 2], h_s), (bank[2 + k % 2], u_s))):
                    pe.matmul(dst, gu_lo[:, m, e, :], x3hi[:, cols], start=True, stop=False)
                    pe.matmul(dst, gu_hi[:, m, e, :], x3lo[:, cols], start=False, stop=False)
                    pe.matmul(dst, gu_hi[:, m, e, :], x3hi[:, cols], start=False, stop=True).then_inc(done, 1)

            def down(k):
                e, c = chunks[k]
                pe.wait_ge(g_s, k + 1)
                if k == 0:
                    pe.wait_ge(dn_l, 32)
                    pe.wait_ge(eneg_s, NT)
                    pe.wait_ge(res2_s, NT)
                if k >= 2:
                    pe.wait_ge(acc_s, TPC * (k - 1))
                for n in range(TPC):
                    last = pe.matmul(bank[4 + k % 2][:, n * D:(n + 1) * D], act[:, k % 3, n * P:(n + 1) * P],
                                     dn_w[:, e, :], start=True, stop=True)
                last.then_inc(y_s, 1)

            for k in range(NK + 2):
                if k < NK:
                    gate_up(k)
                if k >= 2:
                    down(k - 2)


_INS = ["x", "ctx_1024", "L0_attn_w_qkv", "L0_attn_ln_w", "L0_attn_w_proj", "L0_xattn_ln_gamma", "L0_xattn_ln_beta",
        "L0_xattn_w_q", "L0_xattn_w_kv", "L0_xattn_w_out", "L0_xattn_b_out", "L0_xattn_gate", "L0_ffn_router_w",
        "L0_ffn_bias", "L0_ffn_gate_w", "L0_ffn_up_w", "L0_ffn_down_w", "L0_ffn_sh_gate_w", "L0_ffn_sh_up_w",
        "L0_ffn_sh_down_w"]


def kernel(**inputs):
    import numpy as _np
    import concourse.bacc as _bacc
    from concourse import mybir as _mybir
    from concourse.bass_utils import run_bass_kernel_spmd as _run

    nc = _bacc.Bacc("TRN2", target_bir_lowering=False, num_devices=1)
    arrays, args = {}, []
    for name in _INS:
        a = _np.ascontiguousarray(inputs[name])
        arrays[f"in_{name}_dram"] = a
        args.append(nc.dram_tensor(f"in_{name}_dram", a.shape, _mybir.dt.from_np(a.dtype), kind="ExternalInput").ap())
    out = nc.dram_tensor("out_dram", inputs["x"].shape, F32, kind="ExternalOutput").ap()
    decoder_layer(nc, *args, out)
    r = _run(nc, [arrays], core_ids=[0])
    return r.results[0]["out_dram"]
```

```python
from contextlib import ExitStack

import concourse.bass as bass
from concourse import mybir

F32 = mybir.dt.float32
F32R = mybir.dt.float32r
ALU = mybir.AluOpType
ACT = mybir.ActivationFunctionType
AX = mybir.AxisListType

P = 128
QUAD = 32


def decoder_layer(
    nc: bass.Bass,
    x_in: bass.AP,
    ctx_in: bass.AP,
    w_qkv: bass.AP,
    ln_w: bass.AP,
    w_proj: bass.AP,
    gamma: bass.AP,
    beta: bass.AP,
    w_q: bass.AP,
    w_kv: bass.AP,
    w_out: bass.AP,
    b_out: bass.AP,
    gate: bass.AP,
    router_w: bass.AP,
    router_bias: bass.AP,
    gate_w: bass.AP,
    up_w: bass.AP,
    down_w: bass.AP,
    sh_gate_w: bass.AP,
    sh_up_w: bass.AP,
    sh_down_w: bass.AP,
    out: bass.AP,
):
    B, T, D = x_in.shape
    NT = B * T // P
    TPB = T // P
    LS = 32
    HD = 8
    H1 = D // HD
    NR = 4
    NG = P // LS
    HR = H1 // NR
    VA = HR * (HD + 1)
    CTX = ctx_in.shape[1]
    INNER = w_q.shape[1]
    DH = 64
    H2 = INNER // DH
    NPAIR = H2 // 2
    E, _, F = gate_w.shape
    NSH = sh_gate_w.shape[1] // F
    NE = E + NSH
    NGRP = 4
    EPG = E // NGRP
    TOPK = 4
    CHUNK = 512
    NCH = B * T // CHUNK
    TPC = CHUNK // P
    RING = 4
    LN_EPS = 1e-5
    RMS_EPS = 1e-6
    NEG = -3.0e38
    assert D == P and F == P and CTX == 64 and HR == 4 and NR * QUAD == P and LS == QUAD

    with ExitStack() as ctx:
        def sb(name, shape, dt=F32):
            return ctx.enter_context(nc.sbuf_tensor(name, shape, dt))

        def sem(name):
            return ctx.enter_context(nc.semaphore(name))

        bank = [ctx.enter_context(nc.psum_tensor(f"bank{i}", [P, 512], F32)) for i in range(4, 8)]
        wide = ctx.enter_context(nc.psum_tensor("wide", [P, 4, 512], F32))
        bank = [wide[:, i, :] for i in range(4)] + [b[:, :] for b in bank]

        wqkv_sb = sb("wqkv_sb", [P, 3 * D])
        wproj_sb = sb("wproj_sb", [P, D])
        wq_sb = sb("wq_sb", [P, INNER])
        wkv_sb = sb("wkv_sb", [P, 2 * INNER])
        wout_sb = sb("wout_sb", [P, NPAIR, D])
        lnw_col = sb("lnw_col", [P, 1])
        gamma_col = sb("gamma_col", [P, 1])
        beta_col = sb("beta_col", [P, 1])
        row = sb("row", [1, D + E + 1])
        rowb = sb("rowb", [P, D + E + 1])
        rw_sb = sb("rw_sb", [E, D])
        rwT = sb("rwT", [P, E])
        ctx_sb = sb("ctx_sb", [P, 2, D])
        gu_w = sb("gu_w", [P, RING, 2, F])
        gu_hi = sb("gu_hi", [P, RING, 2, F], F32R)
        gu_lo = sb("gu_lo", [P, RING, 2, F], F32R)
        dn_w = sb("dn_w", [P, NE, D])
        ident = sb("ident", [P, P])
        causal = sb("causal", [P, LS])
        headsel = sb("headsel", [P, H1])
        hmask = sb("hmask", [P, HR])
        qmask = sb("qmask", [P, HR])
        half = sb("half", [P, 2])
        tgate = sb("tgate", [P, 1])
        bias_out = sb("bias_out", [1, D])
        ones_row = sb("ones_row", [1, P])
        x = sb("x", [P, NT, D])
        stats = sb("stats", [P, 3, 2, 6])
        mv = sb("mv", [P, 3, NT, 2])
        ve = sb("ve", [P, 3, NT, 1])
        rstd = sb("rstd", [P, 3, NT, 1])
        xn = sb("xn", [P, 3, 2, D])
        xnT = sb("xnT", [P, 2, P])
        sq = sb("sq", [P, 2, D])
        ss = sb("ss", [P, NT, 2])
        ms = sb("ms", [P, NT, 2])
        rqk = sb("rqk", [P, NT, 2])
        qkn = sb("qkn", [P, 2, 2, D])
        qkT = sb("qkT", [P, 2, 2, P])
        kbd = sb("kbd", [P, 2, NG, HR, LS])
        vbd = sb("vbd", [P, 3, NG, NR, HR, HD + 1])
        s1 = sb("s1", [P, 2, H1, LS])
        mx1 = sb("mx1", [P, 2, H1])
        p1 = sb("p1", [P, 2, H1 * LS])
        p1T = sb("p1T", [P, NR, P])
        rs1 = sb("rs1", [P, H1])
        yn = sb("yn", [P, H1, HD])
        yT = sb("yT", [P, P])
        ctxT = sb("ctxT", [P, B, CTX])
        wqT = sb("wqT", [P, NPAIR, D])
        k2 = sb("k2", [P, 2, B, 2, CTX])
        v2 = sb("v2", [P, NPAIR, B, 2, CTX])
        qk_fold = sb("qk_fold", [P, B, NPAIR, 2 * CTX])
        vo_fold = sb("vo_fold", [P, NPAIR, B, D])
        xn2T = sb("xn2T", [P, 2, P])
        s2 = sb("s2", [P, H2, CTX])
        mx2 = sb("mx2", [P, 2, H2])
        p2 = sb("p2", [P, 3, H2, CTX])
        sum2 = sb("sum2", [P, 2, H2])
        rs2 = sb("rs2", [P, 2, H2])
        p2T = sb("p2T", [P, NPAIR, P])
        x3T = sb("x3T", [P, 2, P])
        x3hi = sb("x3hi", [P, NT * P], F32R)
        x3lo = sb("x3lo", [P, NT * P], F32R)
        eneg = sb("eneg", [P, NT, E])
        score = sb("score", [P, NT, E])
        biased = sb("biased", [P, NT, E])
        r_a = sb("r_a", [P, NT, E])
        r_b = sb("r_b", [P, NT, E])
        r_c = sb("r_c", [P, NT, E])
        r_p = sb("r_p", [P, NT, NGRP, 2])
        r_q = sb("r_q", [P, NT, NGRP, 2])
        r_g = sb("r_g", [P, 6, NT, NGRP])
        cmp_a = sb("cmp_a", [P, NT, NGRP, NGRP])
        cmp_b = sb("cmp_b", [P, NT, NGRP, NGRP])
        lower = sb("lower", [P, NGRP, NGRP])
        top8 = sb("top8", [P, NT, 8])
        need = sb("need", [P, NT])
        wsum = sb("wsum", [P, NT])
        combine = sb("combine", [P, NT, NE])
        zero_col = sb("zero_col", [P, 2])
        keep = sb("keep", [P, NT, E])
        nmean = sb("nmean", [P, 3, NT, 1])
        sil = sb("sil", [P, 2, CHUNK])
        act = sb("act", [P, 4, CHUNK])

        x_in_s = [sem(f"x_loaded{i}") for i in range(NT)]
        wqkv_l = sem("wqkv_loaded")
        small_l = sem("small_loaded")
        row_l = sem("row_loaded")
        rw_l = sem("router_loaded")
        ctx_l = sem("ctx_loaded")
        wq_l = sem("wq_loaded")
        wkv_l = sem("wkv_loaded")
        wout_l = sem("wout_loaded")
        wproj_l = sem("wproj_loaded")
        gu_l = [sem(f"gu_loaded{i}") for i in range(RING)]
        dn_l = sem("dn_loaded")
        stored = sem("stored")
        zeroed = sem("zeroed")
        vbd_zero = sem("vbd_zeroed")
        k2_zero = sem("k2_zeroed")
        v2_zero = sem("v2_zeroed")
        late_r = sem("late_constants")
        qmask_r = sem("qmask_ready")
        nm_s = [sem(f"nmean{i}") for i in range(3)]
        ident_r = sem("ident_ready")
        const_r = sem("const_ready")
        headsel_r = sem("headsel_ready")
        hm_r = sem("hmask_ready")
        rowb_r = sem("rowb_ready")
        tg_r = sem("tgate_ready")
        bo_r = sem("bias_out_ready")
        bn_s = [sem(f"bn{i}") for i in range(3)]
        mv_s = [sem(f"mv{i}") for i in range(3)]
        ve_s = [sem(f"ve{i}") for i in range(3)]
        rstd_s = [sem(f"rstd{i}") for i in range(3)]
        xn_s = [sem(f"xn{i}") for i in range(3)]
        xT_s = [sem(f"xT{i}") for i in range(3)]
        xnT_s = sem("xnT_copied")
        qk_s = sem("qk_done")
        v_s = sem("v_done")
        ss_s = sem("squares_summed")
        ms_s = sem("mean_squares")
        rqk_s = sem("rqk")
        qkn_s = sem("qk_normed")
        vbd_s = sem("vbd_copied")
        qkTp_s = sem("qk_transposed")
        qkT_s = sem("qkT_copied")
        kbd_s = sem("kbd_built")
        S1_s = sem("scores1")
        sm1_s = sem("masked1")
        mx1_s = sem("max1")
        sub1_s = sem("sub1")
        p1_s = sem("exp1")
        p1T_s = sem("p1_transposed")
        p1Tc_s = sem("p1T_copied")
        y1_s = sem("pv1")
        rs1_s = sem("rs1")
        yn_s = sem("y_normed")
        yTp_s = sem("y_transposed")
        yT_s = sem("yT_copied")
        o1_s = sem("proj_done")
        res1_s = sem("residual1")
        f_ready = sem("fold_ready")
        f_copied = sem("fold_copied")
        xn2T_s = sem("xn2T_copied")
        S2_s = sem("scores2")
        mx2_s = sem("max2")
        sub2_s = sem("sub2")
        p2_s = sem("exp2")
        sum2_s = sem("sum2")
        rs2_s = sem("rs2")
        pn2_s = sem("p2_normed")
        p2T_s = sem("p2_transposed")
        p2Tc_s = sem("p2T_copied")
        o2_s = sem("out2")
        res2_s = sem("residual2")
        wsplit_hi = sem("w_hi")
        wsplit_lo = sem("w_lo")
        x3T_s = sem("x3T_copied")
        x3hi_s = sem("x3hi")
        x3lo_s = sem("x3lo")
        rwT_p = sem("rw_transposed")
        rwT_s = sem("rwT_copied")
        lg_s = sem("logits")
        eneg_s = sem("exp_logits")
        route = sem("route_step")
        comb_s = sem("combine_ready")
        h_s = sem("h_done")
        u_s = sem("u_done")
        sil_s = sem("silu_done")
        g_s = sem("act_done")
        y_s = sem("down_done")
        acc_s = sem("accumulated")

        T1, QK, FOLD, PV = bank[4], bank[5], bank[6], bank[7]
        VCOL, QKTCOL = P, 2 * P
        OUT2 = bank[5]
        PT2 = [bank[6], bank[7]]

        NK = NE * NCH
        PEEL = NSH * NCH
        TURN = RING * NCH
        TURNS = E // RING

        units_at = {
            0: [("ctx", 0), ("wq", 0), ("wq", 1)], 1: [("kv", 0), ("A", 0), ("kv", 1)],
            2: [("A", 1), ("kv", 2), ("A", 2)], 3: [("kv", 3), ("A", 3)], 4: [("kv", 4), ("A", 4)],
            5: [("kv", 5), ("A", 5)], 6: [("kv", 6), ("A", 6)], 7: [("kv", 7), ("A", 7)],
            8: [("VW", 0), ("VW", 1)], 9: [("VW", 2), ("VW", 3), ("VW", 4)], 10: [("VW", 5), ("VW", 6), ("VW", 7)],
        }
        units = [u for i in sorted(units_at) for u in units_at[i]]
        unit_no = {u: n for n, u in enumerate(units)}
        STEPS = 2 * NT + 4

        def fold_bank(u):
            return QK if u[0] == "VW" and u[1] % 2 == 1 else FOLD

        def units_of(i):
            return units_at.get(i, [])

        block = ctx.enter_context(nc.Block())

        @block.sync
        def _(sp):
            xt = x_in.rearrange("b (n p) d -> (b n) p d", p=P)

            def load_expert(e, slot):
                ed = bass.ds(e, 1)
                sp.dma_start(gu_w[:, slot, 0, :], gate_w[ed].rearrange("e d f -> (e d) f")).then_inc(gu_l[slot], 16)
                sp.dma_start(gu_w[:, slot, 1, :], up_w[ed].rearrange("e d f -> (e d) f")).then_inc(gu_l[slot], 16)

            sp.dma_start(x[:, 0, :], xt[0]).then_inc(x_in_s[0], 16)
            sp.dma_start(wqkv_sb[:, :], w_qkv).then_inc(wqkv_l, 16)
            sp.dma_start(x[:, 1, :], xt[1]).then_inc(x_in_s[1], 16)
            sp.dma_start(lnw_col[:, :], ln_w.rearrange("(p o) -> p o", o=1)).then_inc(small_l, 16)
            sp.dma_start(gamma_col[:, :], gamma.rearrange("(p o) -> p o", o=1)).then_inc(small_l, 16)
            sp.dma_start(beta_col[:, :], beta.rearrange("(p o) -> p o", o=1)).then_inc(small_l, 16)
            sp.dma_start(ctx_sb[:, :, :], ctx_in.rearrange("(n c) s d -> (c s) n d", c=2)).then_inc(ctx_l, 16)
            sp.dma_start(wq_sb[:, :], w_q).then_inc(wq_l, 16)
            sp.dma_start(wkv_sb[:, :], w_kv).then_inc(wkv_l, 16)
            for t in range(2, 4):
                sp.dma_start(x[:, t, :], xt[t]).then_inc(x_in_s[t], 16)
            sp.dma_start(row[:, 0:D], b_out.rearrange("(o d) -> o d", o=1)).then_inc(row_l, 16)
            sp.dma_start(row[:, D:D + E], router_bias.rearrange("(o d) -> o d", o=1)).then_inc(row_l, 16)
            sp.dma_start(row[:, D + E:D + E + 1], gate.rearrange("(o d) -> o d", o=1)).then_inc(row_l, 16)
            for t in range(4, NT):
                sp.dma_start(x[:, t, :], xt[t]).then_inc(x_in_s[t], 16)
            sp.dma_start(wproj_sb[:, :], w_proj).then_inc(wproj_l, 16)
            sp.dma_start(wout_sb[:, :, :], w_out.rearrange("(j p) d -> p j d", p=P)).then_inc(wout_l, 16)
            sp.dma_start(rw_sb[:, :], router_w).then_inc(rw_l, 16)
            for n in range(NSH):
                sp.dma_start(gu_w[:, n, 0, :], sh_gate_w[:, n * F:(n + 1) * F]).then_inc(gu_l[n], 16)
                sp.dma_start(gu_w[:, n, 1, :], sh_up_w[:, n * F:(n + 1) * F]).then_inc(gu_l[n], 16)
            for e in range(RING - NSH):
                load_expert(e, NSH + e)
            sp.dma_start(dn_w[:, 0:NSH, :], sh_down_w.rearrange("(e f) d -> f e d", f=F)).then_inc(dn_l, 16)
            sp.dma_start(dn_w[:, NSH:NE, :], down_w.rearrange("e f d -> f e d")).then_inc(dn_l, 16)
            with sp.Fori(0, TURNS - 1) as it:
                for m in range(RING):
                    sp.wait_ge(wsplit_lo, it * RING + (m + 1))
                    load_expert(it * RING + (RING - NSH + m), m)
            for n in range(TURNS * RING, NE):
                sp.wait_ge(wsplit_lo, n - RING + 1)
                load_expert(n - NSH, n % RING)
            ot = out.rearrange("b (n p) d -> (b n) p d", p=P)
            for t in range(NT):
                sp.wait_ge(acc_s, NT * (NE - 1) + t + 1)
                sp.dma_start(ot[t], x[:, t, :]).then_inc(stored, 16)
            sp.wait_ge(stored, 16 * NT)

        @block.gpsimd
        def _(pool):
            def norm_scale(n, t, scale, eps):
                pool.wait_ge(mv_s[n], t + 1)
                pool.tensor_scalar(ve[:, n, t, :], mv[:, n, t, 1:2], scale, eps, ALU.mult, ALU.add).then_inc(ve_s[n], 1)
                if n > 0:
                    pool.tensor_scalar(nmean[:, n, t, :], mv[:, n, t, 0:1], -1.0, 0.0, ALU.mult, ALU.add).then_inc(nm_s[n], 1)
                pool.wait_ge(ve_s[n], t + 1)
                pool.tensor_tensor(rstd[:, n, t, :], ve[:, n, t, :], half[:, 0:1], ALU.pow).then_inc(rstd_s[n], 1)

            def norm_apply(n, t):
                pool.wait_ge(rstd_s[n], t + 1)
                if t >= 2:
                    pool.wait_ge(xT_s[n], t - 1)
                pool.wait_ge(nm_s[n], t + 1)
                pool.tensor_scalar(xn[:, n, t % 2, :], x[:, t, :], nmean[:, n, t, :], rstd[:, n, t, :],
                                   ALU.add, ALU.mult).then_inc(xn_s[n], 1)

            pool.memset(half[:, :], -0.5).then_inc(zeroed, 1)
            pool.memset(ident[:, :], 0.0).then_inc(zeroed, 1)
            pool.memset(causal[:, :], 0.0).then_inc(zeroed, 1)
            pool.memset(headsel[:, :], 1.0).then_inc(zeroed, 1)
            pool.memset(lower[:, :, :], 1.0).then_inc(zeroed, 1)
            pool.memset(combine[:, :, 0:NSH], 1.0).then_inc(zeroed, 1)
            pool.memset(keep[:, :, :], 1.0).then_inc(zeroed, 1)
            pool.memset(zero_col[:, :], 0.0).then_inc(zeroed, 1)
            pool.memset(qmask[:, :], 0.0).then_inc(zeroed, 1)
            pool.wait_ge(zeroed, 9)
            pool.affine_select(out=ident[:, :], in_=ident[:, :], compare_op=ALU.not_equal, fill=1.0, base=0,
                               pattern=[[-1, P]], channel_multiplier=1).then_inc(ident_r, 1)
            norm_scale(0, 0, 1.0, LN_EPS)
            norm_scale(0, 1, 1.0, LN_EPS)
            pool.affine_select(out=headsel[:, :], in_=headsel[:, :], compare_op=ALU.is_ge, fill=0.0, base=0,
                               pattern=[[-HD, H1]], channel_multiplier=1).then_inc(headsel_r, 1)
            pool.wait_ge(headsel_r, 1)
            pool.affine_select(out=headsel[:, :], in_=headsel[:, :], compare_op=ALU.is_ge, fill=0.0, base=HD - 1,
                               pattern=[[HD, H1]], channel_multiplier=-1).then_inc(headsel_r, 1)
            pool.wait_ge(headsel_r, 2)
            for g in range(NG):
                q = causal[QUAD * g:QUAD * (g + 1), :]
                pool.affine_select(out=q, in_=q, compare_op=ALU.is_ge, fill=NEG, base=0,
                                   pattern=[[-1, LS]], channel_multiplier=1).then_inc(const_r, 1)
                pool.wait_ge(const_r, g + 1)

            for h in range(HR):
                pool.memset(qmask[QUAD * h:QUAD * (h + 1), h:h + 1], 1.0).then_inc(qmask_r, 1)
                pool.wait_ge(qmask_r, h + 1)

            def norm_scale_rest():
                pool.wait_ge(mv_s[0], NT)
                pool.tensor_scalar(ve[:, 0, 2:NT, :], mv[:, 0, 2:NT, 1:2], 1.0, LN_EPS, ALU.mult, ALU.add).then_inc(ve_s[0], 1)
                pool.wait_ge(ve_s[0], 3)
                pool.tensor_tensor(rstd[:, 0, 2:NT, :], ve[:, 0, 2:NT, :],
                                   half[:, 0:1].unsqueeze(1).to_broadcast([P, NT - 2, 1]), ALU.pow).then_inc(rstd_s[0], 1)

            def build_kbd(t):
                pool.wait_ge(qkT_s, t + 1)
                if t == 0:
                    pool.wait_ge(hm_r, 2)
                if t >= 2:
                    pool.wait_ge(S1_s, t - 1)
                pool.tensor_tensor(kbd[:, t % 2, :, :, :],
                                   qkT[:, t % 2, 1, :].rearrange("p (g k) -> p g k", g=NG).unsqueeze(2)
                                   .to_broadcast([P, NG, HR, LS]),
                                   hmask[:, :].unsqueeze(1).unsqueeze(3).to_broadcast([P, NG, HR, LS]),
                                   ALU.mult).then_inc(kbd_s, 1)

            def late_constants():
                pool.affine_select(out=lower[:, :, :], in_=lower[:, :, :], compare_op=ALU.is_gt, fill=0.0, base=0,
                                   pattern=[[1, NGRP], [-1, NGRP]], channel_multiplier=0).then_inc(late_r, 1)
                pool.memset(keep[:, :, 0:1], 0.0).then_inc(late_r, 1)
                pool.memset(ones_row[:, :], 1.0).then_inc(bo_r, 1)
                pool.wait_ge(row_l, 48)
                pool.partition_broadcast(rowb[:, :], row[:, :], P).then_inc(rowb_r, 1)

            def rms(t):
                pool.wait_ge(ss_s, 2 * (t + 1))
                pool.tensor_scalar(ms[:, t, :], ss[:, t, :], 1.0 / D, RMS_EPS, ALU.mult, ALU.add).then_inc(ms_s, 1)
                pool.wait_ge(ms_s, t + 1)
                pool.tensor_tensor(rqk[:, t, :], ms[:, t, :], half[:, :], ALU.pow).then_inc(rqk_s, 1)

            def split_weights(n, slot, turn):
                pool.wait_ge(gu_l[slot], turn * 32 + 32)
                pool.tensor_tensor(gu_hi[:, slot, :, :], gu_w[:, slot, :, :],
                                   zero_col[:, :].unsqueeze(2).to_broadcast([P, 2, F]), ALU.add).then_inc(wsplit_hi, 1)
                pool.wait_ge(wsplit_hi, n + 1)
                pool.tensor_tensor(gu_lo[:, slot, :, :], gu_w[:, slot, :, :], gu_hi[:, slot, :, :].bitcast(F32),
                                   ALU.subtract).then_inc(wsplit_lo, 1)

            def norm_p2(t):
                pool.wait_ge(rs2_s, t + 1)
                pool.tensor_tensor(p2[:, t % 3, :, :], p2[:, t % 3, :, :],
                                   rs2[:, t % 2, :].unsqueeze(2).to_broadcast([P, H2, CTX]),
                                   ALU.mult).then_inc(pn2_s, 1)

            for i in range(STEPS):
                if i < NT:
                    rms(i)
                    if i == 1:
                        norm_scale_rest()
                    build_kbd(i)
                for j in range(3) if i == 0 else range(i + 2, i + 3) if i + 2 < NPAIR else ():
                    pool.memset(v2[:, j, :, :, :], 0.0).then_inc(v2_zero, 1)
                if i == 0:
                    late_constants()
                if i == 2:
                    pool.wait_ge(tg_r, 1)
                    pool.tensor_scalar(bias_out[:, :], row[:, 0:D], tgate[0:1, :], None, ALU.mult).then_inc(bo_r, 1)
                if NT + 1 <= i < NT + 1 + RING // 2:
                    for e in range(2):
                        n = 2 * (i - NT - 1) + e
                        split_weights(n, n, 0)
                if NT + 4 <= i < 2 * NT + 4:
                    norm_scale(2, i - NT - 4, 1.0, LN_EPS)
                    norm_apply(2, i - NT - 4)
                if NT + 2 <= i < 2 * NT + 2:
                    norm_p2(i - NT - 2)
                if NT - 1 <= i < 2 * NT - 1:
                    norm_apply(1, i - NT + 1)
                if 3 <= i < NT + 3:
                    norm_scale(1, i - 3, 1.0 + LN_EPS, LN_EPS * LN_EPS)

            with pool.Fori(0, TURNS - 1) as it:
                for m in range(RING):
                    n = it * RING + (RING + m)
                    pool.wait_ge(u_s, it * TURN + NCH * (m + 1))
                    split_weights(n, m, it + 1)
            for n in range(TURNS * RING, NE):
                pool.wait_ge(u_s, NCH * (n - RING + 1))
                split_weights(n, n % RING, n // RING)

        @block.scalar
        def _(sc):
            def gate_tanh():
                sc.wait_ge(rowb_r, 1)
                sc.activation(tgate[:, :], rowb[:, D + E:D + E + 1], ACT.Tanh).then_inc(tg_r, 1)

            def copy_xnT(t):
                sc.wait_ge(xT_s[0], t + 1)
                if t >= 2:
                    sc.wait_ge(v_s, t - 1)
                sc.copy(xnT[:, t % 2, :], T1[:, 0:P]).then_inc(xnT_s, 1)

            def squares(t):
                sc.wait_ge(qk_s, t + 1)
                for n in range(2):
                    if t >= 1:
                        sc.wait_ge(ss_s, 2 * t)
                    sc.activation(sq[:, n, :], QK[:, n * D:(n + 1) * D], ACT.Square,
                                  accum_out=ss[:, t, n:n + 1]).then_inc(ss_s, 1)

            def scale_qk(t):
                sc.wait_ge(rqk_s, t + 1)
                if t >= 2:
                    sc.wait_ge(qkTp_s, t - 1)
                for n in range(2):
                    sc.activation(qkn[:, t % 2, n, :], QK[:, n * D:(n + 1) * D], ACT.Copy,
                                  scale=rqk[:, t, n:n + 1]).then_inc(qkn_s, 1)

            def copy_qkT(t):
                sc.wait_ge(qkTp_s, t + 1)
                if t == 0:
                    sc.wait_ge(small_l, 48)
                if t >= 2:
                    sc.wait_ge(S1_s, t - 1)
                    sc.wait_ge(kbd_s, t - 1)
                sc.activation(qkT[:, t % 2, :, :].rearrange("p n q -> p (n q)"), T1[:, QKTCOL:QKTCOL + 2 * P], ACT.Copy,
                              scale=lnw_col[:, :]).then_inc(qkT_s, 1)

            def exp1(t):
                sc.wait_ge(sub1_s, t + 1)
                if t >= 2:
                    sc.wait_ge(p1T_s, t - 1)
                sc.activation(p1[:, t % 2, :], s1[:, t % 2, :, :].rearrange("p h k -> p (h k)"), ACT.Exp).then_inc(p1_s, 1)

            def copy_p1T(t):
                sc.wait_ge(p1T_s, t + 1)
                if t >= 1:
                    sc.wait_ge(y1_s, t)
                sc.copy(p1T[:, :, :].rearrange("p r q -> p (r q)"), PV[:, :]).then_inc(p1Tc_s, 1)

            def copy_yT(t):
                sc.wait_ge(yTp_s, t + 1)
                if t >= 1:
                    sc.wait_ge(o1_s, t)
                sc.copy(yT[:, :], PV[:, 2 * P:3 * P]).then_inc(yT_s, 1)

            def copy_fold(u):
                kind, j = u
                n = unit_no[u]
                sc.wait_ge(f_ready, n + 1)
                if kind == "ctx":
                    sc.copy(ctxT[:, :, :].rearrange("p b s -> p (b s)"), FOLD[:, 0:B * CTX]).then_inc(f_copied, 1)
                elif kind == "wq":
                    sc.activation(wqT[:, 4 * j:4 * j + 4, :].rearrange("p j d -> p (j d)"), FOLD[:, :], ACT.Copy,
                                  scale=float(DH) ** -0.5).then_inc(f_copied, 1)
                elif kind == "kv":
                    sc.wait_ge(v2_zero, j + 1)
                    for m, dst in enumerate((k2, v2)):
                        for h in range(2):
                            hs = slice(DH * h, DH * (h + 1))
                            last = sc.copy(dst[hs, j % 2 if m == 0 else j, :, h, :],
                                           FOLD[hs, m * B * CTX:(m + 1) * B * CTX].rearrange("p (b s) -> p b s", b=B))
                    last.then_inc(f_copied, 1)
                elif kind == "A":
                    sc.copy(qk_fold[:, :, j, :], FOLD[:, :].rearrange("p (b s) -> p b s", b=B)).then_inc(f_copied, 1)
                else:
                    sc.activation(vo_fold[:, j, :, :].rearrange("p b d -> p (b d)"), fold_bank(u), ACT.Copy,
                                  scale=tgate[:, :]).then_inc(f_copied, 1)

            def copy_xn2T(t):
                sc.wait_ge(xT_s[1], t + 1)
                if t == 0:
                    sc.wait_ge(small_l, 48)
                if t >= 2:
                    sc.wait_ge(S2_s, t - 1)
                sc.activation(xn2T[:, t % 2, :], T1[:, 0:P], ACT.Identity, scale=gamma_col[:, :],
                              bias=beta_col[:, :]).then_inc(xn2T_s, 1)

            def exp2(t):
                sc.wait_ge(sub2_s, t + 1)
                if t >= 3:
                    sc.wait_ge(p2T_s, t - 2)
                sc.activation(p2[:, t % 3, :, :].rearrange("p h k -> p (h k)"),
                              s2[:, :, :].rearrange("p h k -> p (h k)"), ACT.Exp).then_inc(p2_s, 1)

            def copy_p2T(t):
                for n in range(2):
                    sc.wait_ge(p2T_s, t + 1)
                    if t >= 1:
                        sc.wait_ge(o2_s, t)
                    sc.copy(p2T[:, 4 * n:4 * n + 4, :].rearrange("p j q -> p (j q)"), PT2[n]).then_inc(p2Tc_s, 1)

            def copy_x3T(t):
                sc.wait_ge(xT_s[2], t + 1)
                if t >= 2:
                    sc.wait_ge(x3lo_s, t - 1)
                    sc.wait_ge(lg_s, t - 1)
                sc.copy(x3T[:, t % 2, :], T1[:, P:2 * P]).then_inc(x3T_s, 1)
                sc.wait_ge(x3T_s, t + 1)
                sc.copy(x3hi[:, t * P:(t + 1) * P], x3T[:, t % 2, :]).then_inc(x3hi_s, 1)

            def exp_logits(t):
                sc.wait_ge(lg_s, t + 1)
                sc.activation(eneg[:, t, :], T1[:, 2 * P:2 * P + E], ACT.Exp, scale=-1.0).then_inc(eneg_s, 1)

            copy_xnT(0)
            for i in range(NT):
                us = units_of(i)
                squares(i)
                if i >= 2:
                    exp1(i - 2)
                if i == 1:
                    gate_tanh()
                scale_qk(i)
                if i >= 2:
                    copy_p1T(i - 2)
                copy_fold(us[0])
                copy_qkT(i)
                if i >= 2:
                    copy_yT(i - 2)
                if i + 1 < NT:
                    copy_xnT(i + 1)
                for u in us[1:]:
                    copy_fold(u)
            for i in range(NT, STEPS):
                us = units_of(i)
                if i == NT:
                    exp1(NT - 2)
                if i < NT + 2:
                    copy_p1T(i - 2)
                if i < 2 * NT:
                    copy_xn2T(i - NT)
                for u in us[0:1]:
                    copy_fold(u)
                if i < NT + 2:
                    copy_yT(i - 2)
                if i == NT:
                    exp1(NT - 1)
                for u in us[1:2]:
                    copy_fold(u)
                if NT + 3 <= i < 2 * NT + 3:
                    copy_p2T(i - NT - 3)
                if NT + 4 <= i < 2 * NT + 4:
                    copy_x3T(i - NT - 4)
                if NT + 4 <= i < 2 * NT + 4:
                    exp_logits(i - NT - 4)
                if NT + 1 <= i < 2 * NT + 1:
                    exp2(i - NT - 1)
                for u in us[2:]:
                    copy_fold(u)
                if i == NT + 2:
                    sc.wait_ge(rwT_p, 1)
                    sc.copy(rwT[:, :], T1[:, 3 * P:3 * P + E]).then_inc(rwT_s, 1)

            def silu(k, j):
                sc.wait_ge(h_s, k + 1)
                if j >= 2:
                    sc.wait_ge(g_s, k - 1)
                sc.activation(sil[:, j % 2, :], bank[j % 2], ACT.Silu).then_inc(sil_s, 1)

            for k in range(PEEL):
                silu(k, k)
            with sc.Fori(0, TURNS) as it:
                for j in range(PEEL, PEEL + TURN):
                    silu(it * TURN + j, j)

        @block.vector
        def _(dve):
            def norm_stats(n, t):
                dve.bn_stats(stats[:, n, t % 2, :], x[:, t, :]).then_inc(bn_s[n], 1)
                dve.wait_ge(bn_s[n], t + 1)
                dve.bn_aggr(mv[:, n, t, :], stats[:, n, t % 2, :]).then_inc(mv_s[n], 1)

            def norm_apply(n, t):
                dve.wait_ge(rstd_s[n], min(t + 1, 3))
                if t >= 2:
                    dve.wait_ge(xT_s[n], t - 1)
                dve.tensor_scalar(xn[:, n, t % 2, :], x[:, t, :], mv[:, n, t, 0:1], rstd[:, n, t, :],
                                  ALU.subtract, ALU.mult).then_inc(xn_s[n], 1)

            def build_vbd(t):
                dve.wait_ge(v_s, t + 1)
                if t == 0:
                    dve.wait_ge(qmask_r, HR)
                    dve.wait_ge(vbd_zero, 1 + HR)
                if t >= 3:
                    dve.wait_ge(y1_s, t - 2)
                dve.tensor_tensor(vbd[:, t % 3, :, :, :, 0:HD].rearrange("p g r h d -> p (g r) h d"),
                                  T1[:, VCOL:VCOL + P].rearrange("p (c d) -> p c d", d=HD).unsqueeze(2)
                                  .to_broadcast([P, NG * NR, HR, HD]),
                                  qmask[:, :].unsqueeze(1).unsqueeze(3).to_broadcast([P, NG * NR, HR, HD]),
                                  ALU.mult).then_inc(vbd_s, 1)

            def mask1(t):
                s = s1[:, t % 2, :, :]
                dve.wait_ge(S1_s, t + 1)
                if t == 0:
                    dve.wait_ge(const_r, NG)
                if t >= 2:
                    dve.wait_ge(p1_s, t - 1)
                dve.tensor_tensor(s.rearrange("p (r h) k -> p r h k", r=NR),
                                  wide[:, :, 0:P].rearrange("p r (h k) -> p r h k", h=HR),
                                  causal[:, :].unsqueeze(1).unsqueeze(1).to_broadcast([P, NR, HR, LS]),
                                  ALU.add).then_inc(sm1_s, 1)

            def max1_sub(t):
                s = s1[:, t % 2, :, :]
                dve.wait_ge(sm1_s, t + 1)
                dve.tensor_reduce(mx1[:, t % 2, :], s, AX.X, ALU.max).then_inc(mx1_s, 1)
                dve.wait_ge(mx1_s, t + 1)
                dve.tensor_tensor(s, s, mx1[:, t % 2, :].unsqueeze(2).to_broadcast([P, H1, LS]),
                                  ALU.subtract).then_inc(sub1_s, 1)

            def norm_y(t):
                y = PV[:, 0:NR * VA].rearrange("p (h d) -> p h d", d=HD + 1)
                dve.wait_ge(y1_s, t + 1)
                if t >= 1:
                    dve.wait_ge(yn_s, t)
                dve.reciprocal(rs1[:, :], y[:, :, HD]).then_inc(rs1_s, 1)
                dve.wait_ge(rs1_s, t + 1)
                if t >= 1:
                    dve.wait_ge(yTp_s, t)
                dve.tensor_tensor(yn[:, :, :], y[:, :, 0:HD], rs1[:, :].unsqueeze(2).to_broadcast([P, H1, HD]),
                                  ALU.mult).then_inc(yn_s, 1)

            def residual1(t):
                dve.wait_ge(o1_s, t + 1)
                dve.tensor_tensor(x[:, t, :], PV[:, 3 * P:4 * P], x[:, t, :], ALU.add).then_inc(res1_s, 1)

            def softmax2_max(t):
                s = wide[:, 2 * (t % 2):2 * (t % 2) + 2, :].rearrange("p b (h k) -> p (b h) k", k=CTX)
                dve.wait_ge(S2_s, t + 1)
                if t >= 2:
                    dve.wait_ge(sub2_s, t - 1)
                dve.tensor_reduce(mx2[:, t % 2, :], s, AX.X, ALU.max).then_inc(mx2_s, 1)
                dve.wait_ge(mx2_s, t + 1)
                if t >= 1:
                    dve.wait_ge(p2_s, t)
                dve.tensor_tensor(s2[:, :, :], s, mx2[:, t % 2, :].unsqueeze(2).to_broadcast([P, H2, CTX]),
                                  ALU.subtract).then_inc(sub2_s, 1)

            def softmax2_sum(t):
                dve.wait_ge(p2_s, t + 1)
                dve.tensor_reduce(sum2[:, t % 2, :], p2[:, t % 3, :, :], AX.X, ALU.add).then_inc(sum2_s, 1)
                dve.wait_ge(sum2_s, t + 1)
                if t >= 2:
                    dve.wait_ge(pn2_s, t - 1)
                dve.reciprocal(rs2[:, t % 2, :], sum2[:, t % 2, :]).then_inc(rs2_s, 1)

            def residual2(t):
                dve.wait_ge(o2_s, t + 1)
                dve.wait_ge(xn_s[1], t + 1)
                dve.tensor_tensor(x[:, t, :], OUT2[:, 0:D], x[:, t, :], ALU.add).then_inc(res2_s, 1)

            def split_x3(t):
                dve.wait_ge(x3hi_s, t + 1)
                dve.tensor_tensor(x3lo[:, t * P:(t + 1) * P], x3T[:, t % 2, :],
                                  x3hi[:, t * P:(t + 1) * P].bitcast(F32), ALU.subtract).then_inc(x3lo_s, 1)

            dve.wait_ge(x_in_s[0], 16)
            norm_stats(0, 0)
            dve.wait_ge(x_in_s[1], 16)
            norm_stats(0, 1)
            norm_apply(0, 0)
            dve.memset(vbd[:, :, :, :, :, :], 0.0).then_inc(vbd_zero, 1)
            dve.wait_ge(vbd_zero, 1)
            for h in range(HR):
                dve.memset(vbd[QUAD * h:QUAD * (h + 1), :, :, :, h, HD:HD + 1], 1.0).then_inc(vbd_zero, 1)
            dve.wait_ge(headsel_r, 2)
            dve.tensor_reduce(hmask[:, :], headsel[:, :].rearrange("p (r h) -> p h r", r=NR), AX.X,
                              ALU.add).then_inc(hm_r, 1)
            dve.wait_ge(hm_r, 1)
            dve.tensor_scalar(hmask[:, :], hmask[:, :], float(HD) ** -0.5, None, ALU.mult).then_inc(hm_r, 1)
            for h in range(2):
                dve.memset(k2[DH * h:DH * (h + 1), :, :, 1 - h, :], 0.0).then_inc(k2_zero, 1)
            for i in range(STEPS):
                if i < NT:
                    build_vbd(i)
                if i + 1 < NT:
                    norm_apply(0, i + 1)
                if i == 0:
                    for t in range(2, NT):
                        dve.wait_ge(x_in_s[t], 16)
                        norm_stats(0, t)
                if 1 <= i < NT + 1:
                    mask1(i - 1)
                if 2 <= i < NT + 2:
                    norm_y(i - 2)
                if 1 <= i < NT + 1:
                    max1_sub(i - 1)
                if i == NT + 1:
                    softmax2_max(0)
                if 2 <= i < NT + 2:
                    residual1(i - 2)
                    dve.wait_ge(res1_s, i - 1)
                    norm_stats(1, i - 2)
                if NT + 2 <= i < 2 * NT + 2:
                    softmax2_sum(i - NT - 2)
                if NT + 2 <= i < 2 * NT + 1:
                    softmax2_max(i - NT - 1)
                if NT + 4 <= i < 2 * NT + 4:
                    split_x3(i - NT - 4)
                if NT + 3 <= i < 2 * NT + 3:
                    residual2(i - NT - 3)
                    dve.wait_ge(res2_s, i - NT - 3 + 1)
                    norm_stats(2, i - NT - 3)

            step = [0]

            def then(ins):
                step[0] += 1
                ins.then_inc(route, 1)
                dve.wait_ge(route, step[0])

            ev = [P, NT, E]
            gg = [P, NT, NGRP, NGRP]
            gmax, gmin, lmax, gs, rank, gsel = (r_g[:, n, :, :] for n in range(6))
            by_group = "p t (g a) -> p t g a"

            def group_scores():
                dve.wait_ge(eneg_s, NT)
                dve.wait_ge(late_r, 2)
                then(dve.tensor_scalar(r_a[:, :, :], eneg[:, :, :], 1.0, None, ALU.add))
                then(dve.reciprocal(score[:, :, :], r_a[:, :, :]))
                then(dve.tensor_tensor(biased[:, :, :], score[:, :, :],
                                       rowb[:, D:D + E].unsqueeze(1).to_broadcast(ev), ALU.add))
                pairs = biased[:, :, :].rearrange("p t (g a b) -> p (t g) a b", g=NGRP, a=2)
                hi = r_p[:, :, :, :].rearrange("p t g a -> p (t g) a")
                lo = r_q[:, :, :, :].rearrange("p t g a -> p (t g) a")
                dve.tensor_tensor(hi, pairs[:, :, :, 0], pairs[:, :, :, 1], ALU.max).then_inc(route, 1)
                step[0] += 1
                then(dve.tensor_tensor(lo, pairs[:, :, :, 0], pairs[:, :, :, 1], ALU.min))
                dve.tensor_tensor(gmax, r_p[:, :, :, 0], r_p[:, :, :, 1], ALU.max).then_inc(route, 1)
                dve.tensor_tensor(gmin, r_p[:, :, :, 0], r_p[:, :, :, 1], ALU.min).then_inc(route, 1)
                step[0] += 2
                then(dve.tensor_tensor(lmax, r_q[:, :, :, 0], r_q[:, :, :, 1], ALU.max))
                then(dve.tensor_tensor(lmax, lmax, gmin, ALU.max))
                then(dve.tensor_tensor(gs, gmax, lmax, ALU.add))

            def choose_groups():
                other = gs.unsqueeze(2).to_broadcast(gg)
                own = gs.unsqueeze(3).to_broadcast(gg)
                dve.tensor_tensor(cmp_b[:, :, :, :], other, own, ALU.is_gt).then_inc(route, 1)
                step[0] += 1
                then(dve.tensor_tensor(cmp_a[:, :, :, :], other, own, ALU.is_equal))
                then(dve.tensor_tensor(cmp_a[:, :, :, :], cmp_a[:, :, :, :],
                                       lower[:, :, :].unsqueeze(1).to_broadcast(gg), ALU.mult))
                then(dve.tensor_tensor(cmp_a[:, :, :, :], cmp_a[:, :, :, :], cmp_b[:, :, :, :], ALU.add))
                then(dve.tensor_reduce(rank, cmp_a[:, :, :, :], AX.X, ALU.add))
                then(dve.tensor_scalar(gsel, rank, 1.5, None, ALU.is_lt))
                gsel_e = gsel.unsqueeze(3).to_broadcast([P, NT, NGRP, EPG])
                masked = r_a[:, :, :].rearrange(by_group, g=NGRP)
                then(dve.tensor_tensor(masked, biased[:, :, :].rearrange(by_group, g=NGRP), gsel_e, ALU.mult))
                then(dve.tensor_scalar(gsel, gsel, -1.0, None, ALU.add))
                then(dve.tensor_tensor(masked, masked, gsel_e, ALU.add))

            def choose_experts():
                for t in range(NT):
                    dve.max(top8[:, t, :], r_a[:, t, :]).then_inc(route, 1)
                step[0] += NT
                dve.wait_ge(route, step[0])
                least = top8[:, :, TOPK - 1:TOPK].to_broadcast(ev)
                dve.tensor_tensor(r_b[:, :, :], r_a[:, :, :], least, ALU.is_gt).then_inc(route, 1)
                step[0] += 1
                then(dve.tensor_tensor(biased[:, :, :], r_a[:, :, :], least, ALU.is_equal))
                dve.tensor_reduce(need[:, :], r_b[:, :, :], AX.X, ALU.add).then_inc(route, 1)
                step[0] += 1
                then(dve.tensor_tensor_scan(r_c[:, :, :].rearrange("p t e -> p (t e)"),
                                            keep[:, :, :].rearrange("p t e -> p (t e)"),
                                            biased[:, :, :].rearrange("p t e -> p (t e)"), 0.0, ALU.mult, ALU.add))
                then(dve.tensor_tensor(r_c[:, :, :], r_c[:, :, :], need[:, :].unsqueeze(2).to_broadcast(ev), ALU.add))

            def expert_weights():
                then(dve.tensor_scalar(r_c[:, :, :], r_c[:, :, :], TOPK + 0.5, None, ALU.is_lt))
                then(dve.tensor_tensor(r_c[:, :, :], r_c[:, :, :], biased[:, :, :], ALU.mult))
                then(dve.tensor_tensor(r_b[:, :, :], r_b[:, :, :], r_c[:, :, :], ALU.add))
                then(dve.tensor_tensor(r_b[:, :, :], r_b[:, :, :], score[:, :, :], ALU.mult))
                then(dve.tensor_reduce(wsum[:, :], r_b[:, :, :], AX.X, ALU.add))
                then(dve.tensor_scalar(wsum[:, :], wsum[:, :], 1e-20, None, ALU.add))
                then(dve.reciprocal(wsum[:, :], wsum[:, :]))
                then(dve.tensor_scalar(wsum[:, :], wsum[:, :], 2.5, None, ALU.mult))
                dve.tensor_tensor(combine[:, :, NSH:NE], r_b[:, :, :], wsum[:, :].unsqueeze(2).to_broadcast(ev),
                                  ALU.mult).then_inc(comb_s, 1)

            def multiply(k, j):
                dve.wait_ge(sil_s, k + 1)
                dve.wait_ge(u_s, k + 1)
                if j >= 4:
                    dve.wait_ge(y_s, k - 3)
                dve.tensor_tensor(act[:, j % 4, :], sil[:, j % 2, :], bank[2 + j % 2], ALU.mult).then_inc(g_s, 1)

            def accumulate(k, j, n):
                c = j % NCH
                dve.wait_ge(y_s, k + 1)
                if j >= NCH:
                    dve.wait_ge(acc_s, k * TPC - (NCH - 1) * TPC)
                for m in range(TPC):
                    t = c * TPC + m
                    dve.scalar_tensor_tensor(out=x[:, t, :], in0=bank[4 + j % 4][:, m * D:(m + 1) * D],
                                             scalar=combine[:, t, bass.ds(n, 1)], in1=x[:, t, :],
                                             op0=ALU.mult, op1=ALU.add).then_inc(acc_s, 1)

            parts = (group_scores, choose_groups, choose_experts, expert_weights)
            dve.wait_ge(zeroed, 9)
            for k in range(PEEL):
                parts[k]()
                multiply(k, k)
            for k in range(PEEL - 2):
                accumulate(k, k, k // NCH)
            dve.wait_ge(comb_s, 1)
            with dve.Fori(0, TURNS) as it:
                for j in range(PEEL, PEEL + TURN):
                    multiply(it * TURN + j, j)
                    accumulate(it * TURN + (j - 2), j - 2, it * RING + (j - 2) // NCH)
            for k in range(NK - 2, NK):
                accumulate(k, k, k // NCH)

        @block.tensor
        def _(pe):
            def transpose_xn(n, t, dst):
                pe.wait_ge(xn_s[n], t + 1)
                pe.transpose(dst, xn[:, n, t % 2, :], ident[:, :]).then_inc(xT_s[n], 1)

            def project_qkv(t):
                pe.wait_ge(xnT_s, t + 1)
                if t == 0:
                    pe.wait_ge(wqkv_l, 16)
                if t >= 1:
                    pe.wait_ge(qkn_s, 2 * t)
                pe.matmul(QK[:, 0:2 * D], xnT[:, t % 2, :], wqkv_sb[:, 0:2 * D], start=True, stop=True).then_inc(qk_s, 1)

            def project_v(t):
                for h in range(HR):
                    wv = wqkv_sb[:, 2 * D:3 * D].rearrange("p (r h d) -> p r h d", r=NR, h=HR)[:, :, h, :]
                    for g in range(NG):
                        last = pe.matmul(T1[QUAD * h:QUAD * (h + 1), VCOL + QUAD * g:VCOL + QUAD * (g + 1)],
                                         xnT[:, t % 2, LS * g:LS * (g + 1)], wv, start=True, stop=True)
                last.then_inc(v_s, 1)

            def transpose_qk(t):
                pe.wait_ge(qkn_s, 2 * (t + 1))
                pe.wait_ge(vbd_s, t + 1)
                for n in range(2):
                    last = pe.transpose(T1[:, QKTCOL + n * P:QKTCOL + (n + 1) * P], qkn[:, t % 2, n, :], ident[:, :])
                last.then_inc(qkTp_s, 1)

            def scores1(t):
                pe.wait_ge(qkT_s, t + 1)
                pe.wait_ge(kbd_s, t + 1)
                if t >= 1:
                    pe.wait_ge(sm1_s, t)
                for g in range(NG):
                    for r in range(NR):
                        rows = slice(QUAD * r, QUAD * (r + 1))
                        last = pe.matmul(wide[QUAD * g:QUAD * (g + 1), r, 0:P], qkT[rows, t % 2, 0, LS * g:LS * (g + 1)],
                                         kbd[rows, t % 2, g, :, :].rearrange("p h k -> p (h k)"), start=True, stop=True)
                last.then_inc(S1_s, 1)

            def transpose_p1(t):
                pe.wait_ge(p1_s, t + 1)
                if t >= 1:
                    pe.wait_ge(res1_s, t)
                for r in range(NR):
                    last = pe.transpose(PV[:, r * P:(r + 1) * P], p1[:, t % 2, r * P:(r + 1) * P], ident[:, :])
                last.then_inc(p1T_s, 1)

            def values1(t):
                pe.wait_ge(p1Tc_s, t + 1)
                pe.wait_ge(vbd_s, t + 1)
                for r in range(NR):
                    for g in range(NG):
                        last = pe.matmul(PV[QUAD * g:QUAD * (g + 1), r * VA:(r + 1) * VA],
                                         p1T[:, r, LS * g:LS * (g + 1)],
                                         vbd[:, t % 3, g, r, :, :].rearrange("p h d -> p (h d)"), start=True, stop=True)
                last.then_inc(y1_s, 1)

            def project_y(t):
                pe.wait_ge(yn_s, t + 1)
                pe.transpose(PV[:, 2 * P:3 * P], yn[:, :, :].rearrange("p h d -> p (h d)"), ident[:, :]).then_inc(yTp_s, 1)

            def project_out(t):
                if t == 0:
                    pe.wait_ge(wproj_l, 16)
                pe.wait_ge(yT_s, t + 1)
                pe.matmul(PV[:, 3 * P:4 * P], yT[:, :], wproj_sb[:, :], start=True, stop=True).then_inc(o1_s, 1)

            def fold(u):
                kind, j = u
                n = unit_no[u]
                dst = fold_bank(u)
                if kind == "VW" and j >= 1:
                    pe.wait_ge(f_copied, n - 1)
                elif n >= 1:
                    pe.wait_ge(f_copied, n)
                if kind == "ctx":
                    pe.wait_ge(ctx_l, 16)
                    for m in range(2):
                        last = pe.transpose(FOLD[:, m * P:(m + 1) * P], ctx_sb[:, m, :], ident[:, :])
                elif kind == "wq":
                    pe.wait_ge(wq_l, 16)
                    for m in range(4):
                        last = pe.transpose(FOLD[:, m * P:(m + 1) * P], wq_sb[:, (4 * j + m) * P:(4 * j + m + 1) * P],
                                            ident[:, :])
                elif kind == "kv":
                    pe.wait_ge(wkv_l, 16)
                    for m in range(2):
                        last = pe.matmul(FOLD[:, m * B * CTX:(m + 1) * B * CTX],
                                         wkv_sb[:, m * INNER + j * P:m * INNER + (j + 1) * P],
                                         ctxT[:, :, :].rearrange("p b s -> p (b s)"), start=True, stop=True)
                elif kind == "A":
                    pe.wait_ge(k2_zero, 2)
                    last = pe.matmul(FOLD[:, :], wqT[:, j, :], k2[:, j % 2, :, :, :].rearrange("p b h s -> p (b h s)"),
                                     start=True, stop=True)
                else:
                    pe.wait_ge(wout_l, 16)
                    if j == 1:
                        pe.wait_ge(qkn_s, 2 * NT)
                    for b in range(B):
                        last = pe.matmul(dst[:, b * D:(b + 1) * D], v2[:, j, b, :, :].rearrange("p h s -> p (h s)"),
                                         wout_sb[:, j, :], start=True, stop=True)
                last.then_inc(f_ready, 1)

            def scores2(t):
                b = t // TPB
                pe.wait_ge(xn2T_s, t + 1)
                if t == 0:
                    pe.wait_ge(sm1_s, NT)
                    pe.wait_ge(f_copied, unit_no[("A", NPAIR - 1)] + 1)
                if t >= 2:
                    pe.wait_ge(sub2_s, t - 1)
                fold_b = qk_fold[:, b, :, :].rearrange("p j s -> p (j s)")
                for n in range(2):
                    last = pe.matmul(wide[:, 2 * (t % 2) + n, :], xn2T[:, t % 2, :], fold_b[:, n * 512:(n + 1) * 512],
                                     start=True, stop=True)
                last.then_inc(S2_s, 1)

            def transpose_p2(t):
                pe.wait_ge(pn2_s, t + 1)
                if t == 0:
                    pe.wait_ge(res1_s, NT)
                    pe.wait_ge(f_copied, len(units))
                if t >= 1:
                    pe.wait_ge(p2Tc_s, 2 * t)
                for j in range(NPAIR):
                    last = pe.transpose(PT2[j // 4][:, (j % 4) * P:(j % 4 + 1) * P], p2[:, t % 3, 2 * j:2 * j + 2, :].rearrange("p h k -> p (h k)"),
                                        ident[:, :])
                last.then_inc(p2T_s, 1)

            def output2(t, half_no):
                b = t // TPB
                if half_no == 0:
                    pe.wait_ge(p2Tc_s, 2 * (t + 1))
                    if t == 0:
                        pe.wait_ge(bo_r, 2)
                    if t >= 1:
                        pe.wait_ge(res2_s, t)
                    pe.matmul(OUT2[:, 0:D], ones_row[:, :], bias_out[:, :], start=True, stop=False)
                for j in range(half_no * NPAIR // 2, (half_no + 1) * NPAIR // 2):
                    last = pe.matmul(OUT2[:, 0:D], p2T[:, j, :], vo_fold[:, j, b, :], start=False, stop=(j == NPAIR - 1))
                if half_no == 1:
                    last.then_inc(o2_s, 1)

            def logits(t):
                pe.wait_ge(x3T_s, t + 1)
                pe.matmul(T1[:, 2 * P:2 * P + E], x3T[:, t % 2, :], rwT[:, :], start=True, stop=True).then_inc(lg_s, 1)

            pe.wait_ge(ident_r, 1)
            transpose_xn(0, 0, T1[:, 0:P])
            for i in range(NT):
                us = units_of(i)
                project_qkv(i)
                project_v(i)
                fold(us[0])
                if i >= 2:
                    transpose_p1(i - 2)
                if i >= 1:
                    scores1(i - 1)
                if i >= 2:
                    values1(i - 2)
                transpose_qk(i)
                fold(us[1])
                if i >= 2:
                    project_y(i - 2)
                if i + 1 < NT:
                    pe.wait_ge(qkT_s, i + 1)
                    transpose_xn(0, i + 1, T1[:, 0:P])
                if i >= 2:
                    project_out(i - 2)
                for u in us[2:]:
                    fold(u)

            for i in range(NT, STEPS):
                us = units_of(i)
                if i < NT + 2:
                    transpose_p1(i - 2)
                if i == NT:
                    scores1(NT - 1)
                    pe.wait_ge(qkT_s, NT)
                if i < 2 * NT:
                    if i - NT - 4 > 0:
                        pe.wait_ge(eneg_s, i - NT - 4)
                    elif i == NT + 3:
                        pe.wait_ge(rwT_s, 1)
                    transpose_xn(1, i - NT, T1[:, 0:P])
                for u in us[0:1]:
                    fold(u)
                if i < NT + 2:
                    values1(i - 2)
                if NT + 3 <= i < 2 * NT + 3:
                    transpose_p2(i - NT - 3)
                if i < 2 * NT:
                    scores2(i - NT)
                if i < NT + 2:
                    project_y(i - 2)
                for u in us[1:2]:
                    fold(u)
                if i < NT + 2:
                    project_out(i - 2)
                for u in us[2:]:
                    fold(u)
                if i == NT + 2:
                    pe.wait_ge(rw_l, 16)
                    pe.wait_ge(xn2T_s, 3)
                    pe.transpose(T1[:, 3 * P:3 * P + E], rw_sb[:, :], ident[0:E, 0:E]).then_inc(rwT_p, 1)
                if NT + 4 <= i < 2 * NT + 4:
                    t = i - NT - 4
                    pe.wait_ge(xn2T_s, min(i - NT + 1, NT))
                    if t >= 1:
                        pe.wait_ge(eneg_s, t)
                    transpose_xn(2, t, T1[:, P:2 * P])
                if NT + 3 <= i < 2 * NT + 3:
                    output2(i - NT - 3, 0)
                if NT + 4 <= i < 2 * NT + 4:
                    logits(i - NT - 4)
                if NT + 3 <= i < 2 * NT + 3:
                    output2(i - NT - 3, 1)

            def gate_up(k, j, n):
                c = j % NCH
                slot = (j // NCH) % RING
                pe.wait_ge(wsplit_lo, n + 1)
                if j < NCH:
                    pe.wait_ge(x3lo_s, TPC * (c + 1))
                if j == 0:
                    pe.wait_ge(sub2_s, NT)
                if j >= 2:
                    pe.wait_ge(g_s, k - 1)
                cols = slice(c * CHUNK, (c + 1) * CHUNK)
                for m, (dst, done) in enumerate(((bank[j % 2], h_s), (bank[2 + j % 2], u_s))):
                    pe.matmul(dst, gu_lo[:, slot, m, :], x3hi[:, cols], start=True, stop=False)
                    pe.matmul(dst, gu_hi[:, slot, m, :], x3lo[:, cols], start=False, stop=False)
                    pe.matmul(dst, gu_hi[:, slot, m, :], x3hi[:, cols], start=False, stop=True).then_inc(done, 1)

            def down(k, j, n):
                pe.wait_ge(g_s, k + 1)
                if j == 0:
                    pe.wait_ge(dn_l, 32)
                    pe.wait_ge(eneg_s, NT)
                    pe.wait_ge(res2_s, NT)
                if j >= 4:
                    pe.wait_ge(acc_s, k * TPC - 3 * TPC)
                for m in range(TPC):
                    last = pe.matmul(bank[4 + j % 4][:, m * D:(m + 1) * D], act[:, j % 4, m * P:(m + 1) * P],
                                     dn_w[:, bass.ds(n, 1), :].rearrange("p o d -> p (o d)"), start=True, stop=True)
                last.then_inc(y_s, 1)

            for k in range(PEEL):
                gate_up(k, k, k // NCH)
                if k >= 2:
                    down(k - 2, k - 2, (k - 2) // NCH)
            with pe.Fori(0, TURNS) as it:
                for j in range(PEEL, PEEL + TURN):
                    gate_up(it * TURN + j, j, it * RING + j // NCH)
                    down(it * TURN + (j - 2), j - 2, it * RING + (j - 2) // NCH)
            for k in range(NK - 2, NK):
                down(k, k, k // NCH)


_INS = ["x", "ctx_1024", "L0_attn_w_qkv", "L0_attn_ln_w", "L0_attn_w_proj", "L0_xattn_ln_gamma", "L0_xattn_ln_beta",
        "L0_xattn_w_q", "L0_xattn_w_kv", "L0_xattn_w_out", "L0_xattn_b_out", "L0_xattn_gate", "L0_ffn_router_w",
        "L0_ffn_bias", "L0_ffn_gate_w", "L0_ffn_up_w", "L0_ffn_down_w", "L0_ffn_sh_gate_w", "L0_ffn_sh_up_w",
        "L0_ffn_sh_down_w"]


def kernel(**inputs):
    import numpy as _np
    import concourse.bacc as _bacc
    from concourse import mybir as _mybir
    from concourse.bass_utils import run_bass_kernel_spmd as _run

    nc = _bacc.Bacc("TRN2", target_bir_lowering=False, num_devices=1)
    arrays, args = {}, []
    for name in _INS:
        a = _np.ascontiguousarray(inputs[name])
        arrays[f"in_{name}_dram"] = a
        args.append(nc.dram_tensor(f"in_{name}_dram", a.shape, _mybir.dt.from_np(a.dtype), kind="ExternalInput").ap())
    out = nc.dram_tensor("out_dram", inputs["x"].shape, F32, kind="ExternalOutput").ap()
    decoder_layer(nc, *args, out)
    r = _run(nc, [arrays], core_ids=[0])
    return r.results[0]["out_dram"]
```

```python
from contextlib import ExitStack

import concourse.bass as bass
from concourse import mybir

F32 = mybir.dt.float32
F32R = mybir.dt.float32r
ALU = mybir.AluOpType
ACT = mybir.ActivationFunctionType
AX = mybir.AxisListType

P = 128
QUAD = 32



def decoder_layer(
    nc: bass.Bass,
    x_in: bass.AP,
    ctx_in: bass.AP,
    w_qkv: bass.AP,
    ln_w: bass.AP,
    w_proj: bass.AP,
    gamma: bass.AP,
    beta: bass.AP,
    w_q: bass.AP,
    w_kv: bass.AP,
    w_out: bass.AP,
    b_out: bass.AP,
    gate: bass.AP,
    router_w: bass.AP,
    router_bias: bass.AP,
    gate_w: bass.AP,
    up_w: bass.AP,
    down_w: bass.AP,
    sh_gate_w: bass.AP,
    sh_up_w: bass.AP,
    sh_down_w: bass.AP,
    out: bass.AP,
):
    B, T, D = x_in.shape
    NT = B * T // P
    TPB = T // P
    LS = 32
    HD = 8
    H1 = D // HD
    NR = 4
    NG = P // LS
    HR = H1 // NR
    VA = HR * (HD + 1)
    CTX = ctx_in.shape[1]
    INNER = w_q.shape[1]
    DH = 64
    H2 = INNER // DH
    NPAIR = H2 // 2
    E, _, F = gate_w.shape
    NSH = sh_gate_w.shape[1] // F
    NE = E + NSH
    NGRP = 4
    EPG = E // NGRP
    TOPK = 4
    CHUNK = 512
    NCH = B * T // CHUNK
    TPC = CHUNK // P
    RING = 4
    LN_EPS = 1e-5
    RMS_EPS = 1e-6
    NEG = -3.0e38
    assert D == P and F == P and CTX == 64 and HR == 4 and NR * QUAD == P and LS == QUAD

    with ExitStack() as ctx:
        def sb(name, shape, dt=F32):
            return ctx.enter_context(nc.sbuf_tensor(name, shape, dt))

        def sem(name):
            return ctx.enter_context(nc.semaphore(name))

        bank = [ctx.enter_context(nc.psum_tensor(f"bank{i}", [P, 512], F32)) for i in range(4, 8)]
        wide = ctx.enter_context(nc.psum_tensor("wide", [P, 4, 512], F32))
        bank = [wide[:, i, :] for i in range(4)] + [b[:, :] for b in bank]

        wqkv_sb = sb("wqkv_sb", [P, 3 * D])
        wproj_sb = sb("wproj_sb", [P, D])
        wq_sb = sb("wq_sb", [P, INNER])
        wkv_sb = sb("wkv_sb", [P, 2 * INNER])
        wout_sb = sb("wout_sb", [P, NPAIR, D])
        lnw_col = sb("lnw_col", [P, 1])
        gamma_col = sb("gamma_col", [P, 1])
        beta_col = sb("beta_col", [P, 1])
        row = sb("row", [1, D + E + 1])
        rowb = sb("rowb", [P, D + E + 1])
        rw_sb = sb("rw_sb", [E, D])
        rwT = sb("rwT", [P, E])
        ctx_sb = sb("ctx_sb", [P, 2, D])
        gu_w = sb("gu_w", [P, RING, 2, F])
        gu_hi = sb("gu_hi", [P, RING, 2, F], F32R)
        gu_lo = sb("gu_lo", [P, RING, 2, F], F32R)
        dn_w = sb("dn_w", [P, NE, D])
        ident = sb("ident", [P, P])
        causal = sb("causal", [P, LS])
        headsel = sb("headsel", [P, H1])
        hmask = sb("hmask", [P, HR])
        qmask = sb("qmask", [P, HR])
        half = sb("half", [P, 2])
        tgate = sb("tgate", [P, 1])
        bias_out = sb("bias_out", [1, D])
        ones_row = sb("ones_row", [1, P])
        x = sb("x", [P, NT, D])
        stats = sb("stats", [P, 3, 2, 6])
        mv = sb("mv", [P, 3, NT, 2])
        ve = sb("ve", [P, 3, NT, 1])
        rstd = sb("rstd", [P, 3, NT, 1])
        xn = sb("xn", [P, 3, 2, D])
        xnT = sb("xnT", [P, 2, P])
        sq = sb("sq", [P, 2, D])
        ss = sb("ss", [P, NT, 2])
        ms = sb("ms", [P, NT, 2])
        rqk = sb("rqk", [P, NT, 2])
        qkn = sb("qkn", [P, 2, 2, D])
        qkT = sb("qkT", [P, 2, 2, P])
        kbd = sb("kbd", [P, 2, NG, HR, LS])
        vbd = sb("vbd", [P, 3, NG, NR, HR, HD + 1])
        s1 = sb("s1", [P, 2, H1, LS])
        mx1 = sb("mx1", [P, 2, H1])
        p1 = sb("p1", [P, 2, H1 * LS])
        p1T = sb("p1T", [P, NR, P])
        rs1 = sb("rs1", [P, H1])
        yn = sb("yn", [P, H1, HD])
        yT = sb("yT", [P, P])
        ctxT = sb("ctxT", [P, B, CTX])
        wqT = sb("wqT", [P, NPAIR, D])
        k2 = sb("k2", [P, 2, B, 2, CTX])
        v2 = sb("v2", [P, NPAIR, B, 2, CTX])
        qk_fold = sb("qk_fold", [P, B, NPAIR, 2 * CTX])
        vo_fold = sb("vo_fold", [P, NPAIR, B, D])
        xn2T = sb("xn2T", [P, 2, P])
        s2 = sb("s2", [P, H2, CTX])
        mx2 = sb("mx2", [P, 2, H2])
        p2 = sb("p2", [P, 3, H2, CTX])
        sum2 = sb("sum2", [P, 2, H2])
        rs2 = sb("rs2", [P, 2, H2])
        p2T = sb("p2T", [P, NPAIR, P])
        x3T = sb("x3T", [P, 2, P])
        x3hi = sb("x3hi", [P, NT * P], F32R)
        x3lo = sb("x3lo", [P, NT * P], F32R)
        eneg = sb("eneg", [P, NT, E])
        score = sb("score", [P, NT, E])
        biased = sb("biased", [P, NT, E])
        r_a = sb("r_a", [P, NT, E])
        r_b = sb("r_b", [P, NT, E])
        r_c = sb("r_c", [P, NT, E])
        r_p = sb("r_p", [P, NT, NGRP, 2])
        r_q = sb("r_q", [P, NT, NGRP, 2])
        r_g = sb("r_g", [P, 6, NT, NGRP])
        cmp_a = sb("cmp_a", [P, NT, NGRP, NGRP])
        cmp_b = sb("cmp_b", [P, NT, NGRP, NGRP])
        lower = sb("lower", [P, NGRP, NGRP])
        top8 = sb("top8", [P, NT, 8])
        need = sb("need", [P, NT])
        wsum = sb("wsum", [P, NT])
        combine = sb("combine", [P, NT, E])
        zero_col = sb("zero_col", [P, 2])
        keep = sb("keep", [P, NT, E])
        nmean = sb("nmean", [P, 3, NT, 1])
        sil = sb("sil", [P, 2, CHUNK])
        act = sb("act", [P, 4, CHUNK])

        x_in_s = [sem(f"x_loaded{i}") for i in range(NT)]
        wqkv_l = sem("wqkv_loaded")
        small_l = sem("small_loaded")
        row_l = sem("row_loaded")
        rw_l = sem("router_loaded")
        ctx_l = sem("ctx_loaded")
        wq_l = sem("wq_loaded")
        wkv_l = sem("wkv_loaded")
        wout_l = sem("wout_loaded")
        wproj_l = sem("wproj_loaded")
        gu_l = [sem(f"gu_loaded{i}") for i in range(RING)]
        dn_l = sem("dn_loaded")
        stored = sem("stored")
        zeroed = sem("zeroed")
        vbd_zero = sem("vbd_zeroed")
        k2_zero = sem("k2_zeroed")
        v2_zero = sem("v2_zeroed")
        late_r = sem("late_constants")
        qmask_r = sem("qmask_ready")
        nm_s = [sem(f"nmean{i}") for i in range(3)]
        ident_r = sem("ident_ready")
        const_r = sem("const_ready")
        headsel_r = sem("headsel_ready")
        hm_r = sem("hmask_ready")
        rowb_r = sem("rowb_ready")
        tg_r = sem("tgate_ready")
        bo_r = sem("bias_out_ready")
        bn_s = [sem(f"bn{i}") for i in range(3)]
        mv_s = [sem(f"mv{i}") for i in range(3)]
        ve_s = [sem(f"ve{i}") for i in range(3)]
        rstd_s = [sem(f"rstd{i}") for i in range(3)]
        xn_s = [sem(f"xn{i}") for i in range(3)]
        xT_s = [sem(f"xT{i}") for i in range(3)]
        xnT_s = sem("xnT_copied")
        qk_s = sem("qk_done")
        v_s = sem("v_done")
        ss_s = sem("squares_summed")
        ms_s = sem("mean_squares")
        rqk_s = sem("rqk")
        qkn_s = sem("qk_normed")
        vbd_s = sem("vbd_copied")
        qkTp_s = sem("qk_transposed")
        qkT_s = sem("qkT_copied")
        kbd_s = sem("kbd_built")
        S1_s = sem("scores1")
        sm1_s = sem("masked1")
        mx1_s = sem("max1")
        sub1_s = sem("sub1")
        p1_s = sem("exp1")
        p1T_s = sem("p1_transposed")
        p1Tc_s = sem("p1T_copied")
        y1_s = sem("pv1")
        rs1_s = sem("rs1")
        yn_s = sem("y_normed")
        yTp_s = sem("y_transposed")
        yT_s = sem("yT_copied")
        o1_s = sem("proj_done")
        res1_s = sem("residual1")
        f_ready = sem("fold_ready")
        f_copied = sem("fold_copied")
        xn2T_s = sem("xn2T_copied")
        S2_s = sem("scores2")
        mx2_s = sem("max2")
        sub2_s = sem("sub2")
        p2_s = sem("exp2")
        sum2_s = sem("sum2")
        rs2_s = sem("rs2")
        pn2_s = sem("p2_normed")
        p2T_s = sem("p2_transposed")
        p2Tc_s = sem("p2T_copied")
        o2_s = sem("out2")
        res2_s = sem("residual2")
        wsplit_hi = sem("w_hi")
        wsplit_lo = sem("w_lo")
        x3T_s = sem("x3T_copied")
        x3hi_s = sem("x3hi")
        x3lo_s = sem("x3lo")
        rwT_p = sem("rw_transposed")
        rwT_s = sem("rwT_copied")
        lg_s = sem("logits")
        eneg_s = sem("exp_logits")
        route = sem("route_step")
        comb_s = sem("combine_ready")
        h_s = sem("h_done")
        u_s = sem("u_done")
        sil_s = sem("silu_done")
        g_s = sem("act_done")
        y_s = sem("down_done")
        acc_s = sem("accumulated")

        T1, QK, FOLD, PV = bank[4], bank[5], bank[6], bank[7]
        VCOL, QKTCOL = P, 2 * P
        OUT2 = bank[5]
        PT2 = [bank[6], bank[7]]

        NK = NE * NCH
        PEEL = NSH * NCH
        TURN = RING * NCH
        TURNS = E // RING
        LEAD = PEEL + TURN // 2
        ACC_LAG = PEEL * TPC - NT + (NCH - 1) * TPC

        units_at = {
            0: [("ctx", 0), ("wq", 0), ("wq", 1)], 1: [("kv", 0), ("A", 0)], 2: [("kv", 1), ("A", 1)],
            3: [("kv", 2), ("A", 2)], 4: [("kv", 3), ("A", 3)], 5: [("kv", 4), ("A", 4)], 6: [("kv", 5), ("A", 5)],
            7: [("kv", 6), ("A", 6), ("kv", 7)],
            8: [("A", 7), ("VW", 0)], 9: [("VW", j) for j in range(1, 4)], 10: [("VW", j) for j in range(4, NPAIR)],
        }
        units = [u for i in sorted(units_at) for u in units_at[i]]
        unit_no = {u: n for n, u in enumerate(units)}
        STEPS = 2 * NT + 4

        def fold_bank(u):
            return QK if u[0] == "VW" and u[1] % 2 == 1 else FOLD

        def units_of(i):
            return units_at.get(i, [])

        block = ctx.enter_context(nc.Block())

        @block.sync
        def _(sp):
            xt = x_in.rearrange("b (n p) d -> (b n) p d", p=P)

            def load_expert(e, slot):
                ed = bass.ds(e, 1)
                sp.dma_start(gu_w[:, slot, 0, :], gate_w[ed].rearrange("e d f -> (e d) f")).then_inc(gu_l[slot], 16)
                sp.dma_start(gu_w[:, slot, 1, :], up_w[ed].rearrange("e d f -> (e d) f")).then_inc(gu_l[slot], 16)

            sp.dma_start(x[:, 0, :], xt[0]).then_inc(x_in_s[0], 16)
            sp.dma_start(wqkv_sb[:, :], w_qkv).then_inc(wqkv_l, 16)
            sp.dma_start(x[:, 1, :], xt[1]).then_inc(x_in_s[1], 16)
            sp.dma_start(lnw_col[:, :], ln_w.rearrange("(p o) -> p o", o=1)).then_inc(small_l, 16)
            sp.dma_start(gamma_col[:, :], gamma.rearrange("(p o) -> p o", o=1)).then_inc(small_l, 16)
            sp.dma_start(beta_col[:, :], beta.rearrange("(p o) -> p o", o=1)).then_inc(small_l, 16)
            sp.dma_start(ctx_sb[:, :, :], ctx_in.rearrange("(n c) s d -> (c s) n d", c=2)).then_inc(ctx_l, 16)
            sp.dma_start(wq_sb[:, :], w_q).then_inc(wq_l, 16)
            sp.dma_start(wkv_sb[:, :], w_kv).then_inc(wkv_l, 16)
            for t in range(2, 4):
                sp.dma_start(x[:, t, :], xt[t]).then_inc(x_in_s[t], 16)
            sp.dma_start(row[:, 0:D], b_out.rearrange("(o d) -> o d", o=1)).then_inc(row_l, 16)
            sp.dma_start(row[:, D:D + E], router_bias.rearrange("(o d) -> o d", o=1)).then_inc(row_l, 16)
            sp.dma_start(row[:, D + E:D + E + 1], gate.rearrange("(o d) -> o d", o=1)).then_inc(row_l, 16)
            for t in range(4, NT):
                sp.dma_start(x[:, t, :], xt[t]).then_inc(x_in_s[t], 16)
            sp.dma_start(wproj_sb[:, :], w_proj).then_inc(wproj_l, 16)
            sp.dma_start(wout_sb[:, :, :], w_out.rearrange("(j p) d -> p j d", p=P)).then_inc(wout_l, 16)
            sp.dma_start(rw_sb[:, :], router_w).then_inc(rw_l, 16)
            for n in range(NSH):
                sp.dma_start(gu_w[:, n, 0, :], sh_gate_w[:, n * F:(n + 1) * F]).then_inc(gu_l[n], 16)
                sp.dma_start(gu_w[:, n, 1, :], sh_up_w[:, n * F:(n + 1) * F]).then_inc(gu_l[n], 16)
            for e in range(RING - NSH):
                load_expert(e, NSH + e)
            sp.dma_start(dn_w[:, 0:NSH, :], sh_down_w.rearrange("(e f) d -> f e d", f=F)).then_inc(dn_l, 16)
            sp.dma_start(dn_w[:, NSH:NE, :], down_w.rearrange("e f d -> f e d")).then_inc(dn_l, 16)
            with sp.Fori(0, TURNS - 1) as it:
                for m in range(RING):
                    sp.wait_ge(wsplit_lo, it * RING + (m + 1))
                    load_expert(it * RING + (RING - NSH + m), m)
            for n in range(TURNS * RING, NE):
                sp.wait_ge(wsplit_lo, n - RING + 1)
                load_expert(n - NSH, n % RING)
            ot = out.rearrange("b (n p) d -> (b n) p d", p=P)
            for t in range(NT):
                sp.wait_ge(acc_s, NT * E + t + 1)
                sp.dma_start(ot[t], x[:, t, :]).then_inc(stored, 16)
            sp.wait_ge(stored, 16 * NT)

        def norm_p2(engine, t):
            engine.wait_ge(rs2_s, t + 1)
            engine.tensor_tensor(p2[:, t % 3, :, :], p2[:, t % 3, :, :],
                                 rs2[:, t % 2, :].unsqueeze(2).to_broadcast([P, H2, CTX]), ALU.mult).then_inc(pn2_s, 1)

        @block.gpsimd
        def _(pool):
            def norm_scale(n, t, scale, eps):
                pool.wait_ge(mv_s[n], t + 1)
                pool.tensor_scalar(ve[:, n, t, :], mv[:, n, t, 1:2], scale, eps, ALU.mult, ALU.add).then_inc(ve_s[n], 1)
                if n > 0:
                    pool.tensor_scalar(nmean[:, n, t, :], mv[:, n, t, 0:1], -1.0, 0.0,
                                       ALU.mult, ALU.add).then_inc(nm_s[n], 1)
                pool.wait_ge(ve_s[n], t + 1)
                pool.tensor_tensor(rstd[:, n, t, :], ve[:, n, t, :], half[:, 0:1], ALU.pow).then_inc(rstd_s[n], 1)

            def norm_apply(n, t):
                pool.wait_ge(rstd_s[n], t + 1)
                if t >= 2:
                    pool.wait_ge(xT_s[n], t - 1)
                pool.wait_ge(nm_s[n], t + 1)
                pool.tensor_scalar(xn[:, n, t % 2, :], x[:, t, :], nmean[:, n, t, :], rstd[:, n, t, :],
                                   ALU.add, ALU.mult).then_inc(xn_s[n], 1)

            pool.memset(half[:, :], -0.5).then_inc(zeroed, 1)
            pool.memset(ident[:, :], 0.0).then_inc(zeroed, 1)
            pool.memset(causal[:, :], 0.0).then_inc(zeroed, 1)
            pool.memset(headsel[:, :], 1.0).then_inc(zeroed, 1)
            pool.memset(lower[:, :, :], 1.0).then_inc(zeroed, 1)
            pool.memset(keep[:, :, :], 1.0).then_inc(zeroed, 1)
            pool.memset(zero_col[:, :], 0.0).then_inc(zeroed, 1)
            pool.memset(qmask[:, :], 0.0).then_inc(zeroed, 1)
            pool.wait_ge(zeroed, 8)
            pool.affine_select(out=ident[:, :], in_=ident[:, :], compare_op=ALU.not_equal, fill=1.0, base=0,
                               pattern=[[-1, P]], channel_multiplier=1).then_inc(ident_r, 1)
            norm_scale(0, 0, 1.0, LN_EPS)
            norm_scale(0, 1, 1.0, LN_EPS)
            pool.affine_select(out=headsel[:, :], in_=headsel[:, :], compare_op=ALU.is_ge, fill=0.0, base=0,
                               pattern=[[-HD, H1]], channel_multiplier=1).then_inc(headsel_r, 1)
            pool.wait_ge(headsel_r, 1)
            pool.affine_select(out=headsel[:, :], in_=headsel[:, :], compare_op=ALU.is_ge, fill=0.0, base=HD - 1,
                               pattern=[[HD, H1]], channel_multiplier=-1).then_inc(headsel_r, 1)
            pool.wait_ge(headsel_r, 2)
            for g in range(NG):
                q = causal[QUAD * g:QUAD * (g + 1), :]
                pool.affine_select(out=q, in_=q, compare_op=ALU.is_ge, fill=NEG, base=0,
                                   pattern=[[-1, LS]], channel_multiplier=1).then_inc(const_r, 1)
                pool.wait_ge(const_r, g + 1)

            for h in range(HR):
                pool.memset(qmask[QUAD * h:QUAD * (h + 1), h:h + 1], 1.0).then_inc(qmask_r, 1)
                pool.wait_ge(qmask_r, h + 1)

            def norm_scale_rest():
                pool.wait_ge(mv_s[0], NT)
                pool.tensor_scalar(ve[:, 0, 3:NT, :], mv[:, 0, 3:NT, 1:2], 1.0, LN_EPS,
                                   ALU.mult, ALU.add).then_inc(ve_s[0], 1)
                pool.wait_ge(ve_s[0], 4)
                pool.tensor_tensor(rstd[:, 0, 3:NT, :], ve[:, 0, 3:NT, :],
                                   half[:, 0:1].unsqueeze(1).to_broadcast([P, NT - 3, 1]),
                                   ALU.pow).then_inc(rstd_s[0], 1)

            def build_kbd(t):
                pool.wait_ge(qkT_s, t + 1)
                if t == 0:
                    pool.wait_ge(hm_r, 2)
                if t >= 2:
                    pool.wait_ge(S1_s, t - 1)
                pool.tensor_tensor(kbd[:, t % 2, :, :, :],
                                   qkT[:, t % 2, 1, :].rearrange("p (g k) -> p g k", g=NG).unsqueeze(2)
                                   .to_broadcast([P, NG, HR, LS]),
                                   hmask[:, :].unsqueeze(1).unsqueeze(3).to_broadcast([P, NG, HR, LS]),
                                   ALU.mult).then_inc(kbd_s, 1)

            def late_constants():
                pool.affine_select(out=lower[:, :, :], in_=lower[:, :, :], compare_op=ALU.is_gt, fill=0.0, base=0,
                                   pattern=[[1, NGRP], [-1, NGRP]], channel_multiplier=0).then_inc(late_r, 1)
                pool.memset(keep[:, :, 0:1], 0.0).then_inc(late_r, 1)
                pool.memset(ones_row[:, :], 1.0).then_inc(bo_r, 1)
                pool.wait_ge(row_l, 48)
                pool.partition_broadcast(rowb[:, :], row[:, :], P).then_inc(rowb_r, 1)

            def rms(t):
                pool.wait_ge(ss_s, 2 * (t + 1))
                pool.tensor_scalar(ms[:, t, :], ss[:, t, :], 1.0 / D, RMS_EPS, ALU.mult, ALU.add).then_inc(ms_s, 1)
                pool.wait_ge(ms_s, t + 1)
                pool.tensor_tensor(rqk[:, t, :], ms[:, t, :], half[:, :], ALU.pow).then_inc(rqk_s, 1)

            def split_weights(n, slot, turn):
                pool.wait_ge(gu_l[slot], turn * 32 + 32)
                pool.tensor_tensor(gu_hi[:, slot, :, :], gu_w[:, slot, :, :],
                                   zero_col[:, :].unsqueeze(2).to_broadcast([P, 2, F]), ALU.add).then_inc(wsplit_hi, 1)
                pool.wait_ge(wsplit_hi, n + 1)
                pool.tensor_tensor(gu_lo[:, slot, :, :], gu_w[:, slot, :, :], gu_hi[:, slot, :, :].bitcast(F32),
                                   ALU.subtract).then_inc(wsplit_lo, 1)

            for i in range(STEPS):
                if i < NT:
                    rms(i)
                    if i == 1:
                        norm_scale(0, 2, 1.0, LN_EPS)
                    build_kbd(i)
                    if i == 1:
                        norm_scale_rest()
                for j in range(3) if i == 0 else range(i + 2, i + 3) if i + 2 < NPAIR else ():
                    pool.memset(v2[:, j, :, :, :], 0.0).then_inc(v2_zero, 1)
                if i == 0:
                    late_constants()
                if i == 2:
                    pool.wait_ge(tg_r, 1)
                    pool.tensor_scalar(bias_out[:, :], row[:, 0:D], tgate[0:1, :], None, ALU.mult).then_inc(bo_r, 1)
                if NT + 1 <= i < NT + 1 + RING // 2:
                    for e in range(2):
                        n = 2 * (i - NT - 1) + e
                        split_weights(n, n, 0)
                if NT + 4 <= i < 2 * NT + 4:
                    norm_scale(2, i - NT - 4, 1.0, LN_EPS)
                    norm_apply(2, i - NT - 4)
                if NT - 1 <= i < 2 * NT - 1:
                    norm_apply(1, i - NT + 1)
                if NT + 2 <= i < 2 * NT + 1:
                    norm_p2(pool, i - NT - 2)
                if 3 <= i < NT + 3:
                    norm_scale(1, i - 3, 1.0 + LN_EPS, LN_EPS * LN_EPS)

            with pool.Fori(0, TURNS - 1) as it:
                for m in range(RING):
                    n = it * RING + (RING + m)
                    pool.wait_ge(u_s, it * TURN + NCH * (m + 1))
                    split_weights(n, m, it + 1)
            for n in range(TURNS * RING, NE):
                pool.wait_ge(u_s, NCH * (n - RING + 1))
                split_weights(n, n % RING, n // RING)

        @block.scalar
        def _(sc):
            def gate_tanh():
                sc.wait_ge(rowb_r, 1)
                sc.activation(tgate[:, :], rowb[:, D + E:D + E + 1], ACT.Tanh).then_inc(tg_r, 1)

            def copy_xnT(t):
                sc.wait_ge(xT_s[0], t + 1)
                if t >= 2:
                    sc.wait_ge(v_s, t - 1)
                sc.copy(xnT[:, t % 2, :], T1[:, 0:P]).then_inc(xnT_s, 1)

            def squares(t):
                sc.wait_ge(qk_s, t + 1)
                for n in range(2):
                    if t >= 1:
                        sc.wait_ge(ss_s, 2 * t)
                    sc.activation(sq[:, n, :], QK[:, n * D:(n + 1) * D], ACT.Square,
                                  accum_out=ss[:, t, n:n + 1]).then_inc(ss_s, 1)

            def scale_qk(t):
                sc.wait_ge(rqk_s, t + 1)
                if t >= 2:
                    sc.wait_ge(qkTp_s, t - 1)
                for n in range(2):
                    sc.activation(qkn[:, t % 2, n, :], QK[:, n * D:(n + 1) * D], ACT.Copy,
                                  scale=rqk[:, t, n:n + 1]).then_inc(qkn_s, 1)

            def copy_qkT(t):
                sc.wait_ge(qkTp_s, t + 1)
                if t == 0:
                    sc.wait_ge(small_l, 48)
                if t >= 2:
                    sc.wait_ge(S1_s, t - 1)
                    sc.wait_ge(kbd_s, t - 1)
                sc.activation(qkT[:, t % 2, :, :].rearrange("p n q -> p (n q)"), T1[:, QKTCOL:QKTCOL + 2 * P], ACT.Copy,
                              scale=lnw_col[:, :]).then_inc(qkT_s, 1)

            def exp1(t):
                sc.wait_ge(sub1_s, t + 1)
                if t >= 2:
                    sc.wait_ge(p1T_s, t - 1)
                sc.activation(p1[:, t % 2, :], s1[:, t % 2, :, :].rearrange("p h k -> p (h k)"),
                              ACT.Exp).then_inc(p1_s, 1)

            def copy_p1T(t):
                sc.wait_ge(p1T_s, t + 1)
                if t >= 1:
                    sc.wait_ge(y1_s, t)
                sc.copy(p1T[:, :, :].rearrange("p r q -> p (r q)"), PV[:, :]).then_inc(p1Tc_s, 1)

            def copy_yT(t):
                sc.wait_ge(yTp_s, t + 1)
                if t >= 1:
                    sc.wait_ge(o1_s, t)
                sc.copy(yT[:, :], PV[:, 2 * P:3 * P]).then_inc(yT_s, 1)

            def copy_fold(u):
                kind, j = u
                n = unit_no[u]
                sc.wait_ge(f_ready, n + 1)
                if kind == "ctx":
                    sc.copy(ctxT[:, :, :].rearrange("p b s -> p (b s)"), FOLD[:, 0:B * CTX]).then_inc(f_copied, 1)
                elif kind == "wq":
                    sc.activation(wqT[:, 4 * j:4 * j + 4, :].rearrange("p j d -> p (j d)"), FOLD[:, :], ACT.Copy,
                                  scale=float(DH) ** -0.5).then_inc(f_copied, 1)
                elif kind == "kv":
                    sc.wait_ge(v2_zero, j + 1)
                    for m, dst in enumerate((k2, v2)):
                        for h in range(2):
                            hs = slice(DH * h, DH * (h + 1))
                            last = sc.copy(dst[hs, j % 2 if m == 0 else j, :, h, :],
                                           FOLD[hs, m * B * CTX:(m + 1) * B * CTX].rearrange("p (b s) -> p b s", b=B))
                    last.then_inc(f_copied, 1)
                elif kind == "A":
                    sc.copy(qk_fold[:, :, j, :], FOLD[:, :].rearrange("p (b s) -> p b s", b=B)).then_inc(f_copied, 1)
                else:
                    sc.activation(vo_fold[:, j, :, :].rearrange("p b d -> p (b d)"), fold_bank(u), ACT.Copy,
                                  scale=tgate[:, :]).then_inc(f_copied, 1)

            def copy_xn2T(t):
                sc.wait_ge(xT_s[1], t + 1)
                if t == 0:
                    sc.wait_ge(small_l, 48)
                if t >= 2:
                    sc.wait_ge(S2_s, t - 1)
                sc.activation(xn2T[:, t % 2, :], T1[:, 0:P], ACT.Identity, scale=gamma_col[:, :],
                              bias=beta_col[:, :]).then_inc(xn2T_s, 1)

            def exp2(t):
                sc.wait_ge(sub2_s, t + 1)
                if t >= 3:
                    sc.wait_ge(p2T_s, 2 * (t - 2))
                sc.activation(p2[:, t % 3, :, :].rearrange("p h k -> p (h k)"),
                              s2[:, :, :].rearrange("p h k -> p (h k)"), ACT.Exp).then_inc(p2_s, 1)

            def copy_p2T(t):
                for n in range(2):
                    sc.wait_ge(p2T_s, 2 * t + n + 1)
                    if t >= 1:
                        sc.wait_ge(o2_s, t)
                    sc.copy(p2T[:, 4 * n:4 * n + 4, :].rearrange("p j q -> p (j q)"), PT2[n]).then_inc(p2Tc_s, 1)

            def copy_x3T(t):
                sc.wait_ge(xT_s[2], t + 1)
                if t >= 2:
                    sc.wait_ge(x3lo_s, t - 1)
                    sc.wait_ge(lg_s, t - 1)
                sc.copy(x3T[:, t % 2, :], T1[:, P:2 * P]).then_inc(x3T_s, 1)
                sc.wait_ge(x3T_s, t + 1)
                sc.copy(x3hi[:, t * P:(t + 1) * P], x3T[:, t % 2, :]).then_inc(x3hi_s, 1)

            def exp_logits(t):
                sc.wait_ge(lg_s, t + 1)
                sc.activation(eneg[:, t, :], T1[:, 2 * P:2 * P + E], ACT.Exp, scale=-1.0).then_inc(eneg_s, 1)

            copy_xnT(0)
            for i in range(NT):
                us = units_of(i)
                squares(i)
                if i >= 2:
                    exp1(i - 2)
                if i == 1:
                    gate_tanh()
                scale_qk(i)
                if i >= 2:
                    copy_p1T(i - 2)
                copy_fold(us[0])
                copy_qkT(i)
                if i + 1 < NT:
                    copy_xnT(i + 1)
                if i >= 2:
                    copy_yT(i - 2)
                copy_fold(us[1])
                if i == NT - 1:
                    exp1(NT - 2)
                for u in us[2:]:
                    copy_fold(u)
            for i in range(NT, STEPS):
                us = units_of(i)
                if i < NT + 2:
                    copy_p1T(i - 2)
                if i == NT:
                    copy_xn2T(0)
                for u in us[0:1]:
                    copy_fold(u)
                if i < NT + 2:
                    copy_yT(i - 2)
                if i == NT:
                    exp1(NT - 1)
                for u in us[1:2]:
                    copy_fold(u)
                if NT + 3 <= i < 2 * NT + 3:
                    copy_p2T(i - NT - 3)
                if NT + 4 <= i < 2 * NT + 4:
                    copy_x3T(i - NT - 4)
                if i < NT + 3:
                    if NT + 1 <= i:
                        exp2(i - NT - 1)
                    for u in us[2:]:
                        copy_fold(u)
                if i < 2 * NT - 1:
                    copy_xn2T(i - NT + 1)
                if i == NT + 1:
                    sc.wait_ge(rwT_p, 1)
                    sc.copy(rwT[:, :], T1[:, 3 * P:3 * P + E]).then_inc(rwT_s, 1)
                if NT + 4 <= i < 2 * NT + 4:
                    exp_logits(i - NT - 4)
                if NT + 3 <= i < 2 * NT + 1:
                    exp2(i - NT - 1)

            def silu(k, j):
                sc.wait_ge(h_s, k + 1)
                if j >= 2:
                    sc.wait_ge(g_s, k - 1)
                sc.activation(sil[:, j % 2, :], bank[j % 2], ACT.Silu).then_inc(sil_s, 1)

            for k in range(PEEL):
                silu(k, k)
            with sc.Fori(0, TURNS) as it:
                for j in range(PEEL, PEEL + TURN):
                    silu(it * TURN + j, j)

        @block.vector
        def _(dve):
            def norm_stats(n, t):
                if n > 0:
                    dve.wait_ge((res1_s, res2_s)[n - 1], t + 1)
                dve.bn_stats(stats[:, n, t % 2, :], x[:, t, :]).then_inc(bn_s[n], 1)
                dve.wait_ge(bn_s[n], t + 1)
                dve.bn_aggr(mv[:, n, t, :], stats[:, n, t % 2, :]).then_inc(mv_s[n], 1)

            def norm_apply(n, t):
                dve.wait_ge(rstd_s[n], min(t + 1, 4))
                if t >= 2:
                    dve.wait_ge(xT_s[n], t - 1)
                dve.tensor_scalar(xn[:, n, t % 2, :], x[:, t, :], mv[:, n, t, 0:1], rstd[:, n, t, :],
                                  ALU.subtract, ALU.mult).then_inc(xn_s[n], 1)

            def build_vbd(t):
                dve.wait_ge(v_s, t + 1)
                if t == 0:
                    dve.wait_ge(qmask_r, HR)
                    dve.wait_ge(vbd_zero, 1 + HR)
                if t >= 3:
                    dve.wait_ge(y1_s, t - 2)
                dve.tensor_tensor(vbd[:, t % 3, :, :, :, 0:HD].rearrange("p g r h d -> p (g r) h d"),
                                  T1[:, VCOL:VCOL + P].rearrange("p (c d) -> p c d", d=HD).unsqueeze(2)
                                  .to_broadcast([P, NG * NR, HR, HD]),
                                  qmask[:, :].unsqueeze(1).unsqueeze(3).to_broadcast([P, NG * NR, HR, HD]),
                                  ALU.mult).then_inc(vbd_s, 1)

            def mask1(t):
                s = s1[:, t % 2, :, :]
                dve.wait_ge(S1_s, t + 1)
                if t == 0:
                    dve.wait_ge(const_r, NG)
                if t >= 2:
                    dve.wait_ge(p1_s, t - 1)
                dve.tensor_tensor(s.rearrange("p (r h) k -> p r h k", r=NR),
                                  wide[:, :, 0:P].rearrange("p r (h k) -> p r h k", h=HR),
                                  causal[:, :].unsqueeze(1).unsqueeze(1).to_broadcast([P, NR, HR, LS]),
                                  ALU.add).then_inc(sm1_s, 1)

            def max1_sub(t):
                s = s1[:, t % 2, :, :]
                dve.wait_ge(sm1_s, t + 1)
                dve.tensor_reduce(mx1[:, t % 2, :], s, AX.X, ALU.max).then_inc(mx1_s, 1)
                dve.wait_ge(mx1_s, t + 1)
                dve.tensor_tensor(s, s, mx1[:, t % 2, :].unsqueeze(2).to_broadcast([P, H1, LS]),
                                  ALU.subtract).then_inc(sub1_s, 1)

            def norm_y(t):
                y = PV[:, 0:NR * VA].rearrange("p (h d) -> p h d", d=HD + 1)
                dve.wait_ge(y1_s, t + 1)
                if t >= 1:
                    dve.wait_ge(yn_s, t)
                dve.reciprocal(rs1[:, :], y[:, :, HD]).then_inc(rs1_s, 1)
                dve.wait_ge(rs1_s, t + 1)
                if t >= 1:
                    dve.wait_ge(yTp_s, t)
                dve.tensor_tensor(yn[:, :, :], y[:, :, 0:HD], rs1[:, :].unsqueeze(2).to_broadcast([P, H1, HD]),
                                  ALU.mult).then_inc(yn_s, 1)

            def residual1(t):
                dve.wait_ge(o1_s, t + 1)
                dve.tensor_tensor(x[:, t, :], PV[:, 3 * P:4 * P], x[:, t, :], ALU.add).then_inc(res1_s, 1)

            def softmax2_max(t):
                s = wide[:, 2 * (t % 2):2 * (t % 2) + 2, :].rearrange("p b (h k) -> p (b h) k", k=CTX)
                dve.wait_ge(S2_s, t + 1)
                if t >= 2:
                    dve.wait_ge(sub2_s, t - 1)
                dve.tensor_reduce(mx2[:, t % 2, :], s, AX.X, ALU.max).then_inc(mx2_s, 1)
                dve.wait_ge(mx2_s, t + 1)
                if t >= 1:
                    dve.wait_ge(p2_s, t)
                dve.tensor_tensor(s2[:, :, :], s, mx2[:, t % 2, :].unsqueeze(2).to_broadcast([P, H2, CTX]),
                                  ALU.subtract).then_inc(sub2_s, 1)

            def softmax2_sum(t):
                dve.wait_ge(p2_s, t + 1)
                dve.tensor_reduce(sum2[:, t % 2, :], p2[:, t % 3, :, :], AX.X, ALU.add).then_inc(sum2_s, 1)
                dve.wait_ge(sum2_s, t + 1)
                if t >= 2:
                    dve.wait_ge(pn2_s, t - 1)
                dve.reciprocal(rs2[:, t % 2, :], sum2[:, t % 2, :]).then_inc(rs2_s, 1)
                if t == NT - 1:
                    dve.wait_ge(pn2_s, t)
                    norm_p2(dve, t)

            def residual2(t):
                dve.wait_ge(o2_s, t + 1)
                dve.wait_ge(xn_s[1], t + 1)
                dve.tensor_tensor(x[:, t, :], OUT2[:, 0:D], x[:, t, :], ALU.add).then_inc(res2_s, 1)

            def split_x3(t):
                dve.wait_ge(x3hi_s, t + 1)
                dve.tensor_tensor(x3lo[:, t * P:(t + 1) * P], x3T[:, t % 2, :],
                                  x3hi[:, t * P:(t + 1) * P].bitcast(F32), ALU.subtract).then_inc(x3lo_s, 1)

            step = [0]

            def then(ins):
                step[0] += 1
                ins.then_inc(route, 1)
                dve.wait_ge(route, step[0])

            def views(ts):
                return (r_g[:, n, ts, :] for n in range(6))

            by_group = "p t (g a) -> p t g a"

            def group_scores(ts):
                dve.wait_ge(eneg_s, ts.stop)
                gmax, gmin, lmax, gs, rank, gsel = views(ts)
                ev = [P, ts.stop - ts.start, E]
                dve.wait_ge(late_r, 2)
                then(dve.tensor_scalar(r_a[:, ts, :], eneg[:, ts, :], 1.0, None, ALU.add))
                then(dve.reciprocal(score[:, ts, :], r_a[:, ts, :]))
                then(dve.tensor_tensor(biased[:, ts, :], score[:, ts, :],
                                       rowb[:, D:D + E].unsqueeze(1).to_broadcast(ev), ALU.add))
                pairs = biased[:, ts, :].rearrange("p t (g a b) -> p (t g) a b", g=NGRP, a=2)
                hi = r_p[:, ts, :, :].rearrange("p t g a -> p (t g) a")
                lo = r_q[:, ts, :, :].rearrange("p t g a -> p (t g) a")
                dve.tensor_tensor(hi, pairs[:, :, :, 0], pairs[:, :, :, 1], ALU.max).then_inc(route, 1)
                step[0] += 1
                then(dve.tensor_tensor(lo, pairs[:, :, :, 0], pairs[:, :, :, 1], ALU.min))
                dve.tensor_tensor(gmax, r_p[:, ts, :, 0], r_p[:, ts, :, 1], ALU.max).then_inc(route, 1)
                dve.tensor_tensor(gmin, r_p[:, ts, :, 0], r_p[:, ts, :, 1], ALU.min).then_inc(route, 1)
                step[0] += 2
                then(dve.tensor_tensor(lmax, r_q[:, ts, :, 0], r_q[:, ts, :, 1], ALU.max))
                then(dve.tensor_tensor(lmax, lmax, gmin, ALU.max))
                then(dve.tensor_tensor(gs, gmax, lmax, ALU.add))

            def choose_groups(ts):
                gmax, gmin, lmax, gs, rank, gsel = views(ts)
                n_tiles = ts.stop - ts.start
                gg = [P, n_tiles, NGRP, NGRP]
                other = gs.unsqueeze(2).to_broadcast(gg)
                own = gs.unsqueeze(3).to_broadcast(gg)
                dve.tensor_tensor(cmp_b[:, ts, :, :], other, own, ALU.is_gt).then_inc(route, 1)
                step[0] += 1
                then(dve.tensor_tensor(cmp_a[:, ts, :, :], other, own, ALU.is_equal))
                then(dve.tensor_tensor(cmp_a[:, ts, :, :], cmp_a[:, ts, :, :],
                                       lower[:, :, :].unsqueeze(1).to_broadcast(gg), ALU.mult))
                then(dve.tensor_tensor(cmp_a[:, ts, :, :], cmp_a[:, ts, :, :], cmp_b[:, ts, :, :], ALU.add))
                then(dve.tensor_reduce(rank, cmp_a[:, ts, :, :], AX.X, ALU.add))
                then(dve.tensor_scalar(gsel, rank, 1.5, None, ALU.is_lt))
                gsel_e = gsel.unsqueeze(3).to_broadcast([P, n_tiles, NGRP, EPG])
                masked = r_a[:, ts, :].rearrange(by_group, g=NGRP)
                then(dve.tensor_tensor(masked, biased[:, ts, :].rearrange(by_group, g=NGRP), gsel_e, ALU.mult))
                then(dve.tensor_scalar(gsel, gsel, -1.0, None, ALU.add))
                then(dve.tensor_tensor(masked, masked, gsel_e, ALU.add))

            def choose_experts(ts):
                for t in range(ts.start, ts.stop):
                    dve.max(top8[:, t, :], r_a[:, t, :]).then_inc(route, 1)
                step[0] += ts.stop - ts.start
                dve.wait_ge(route, step[0])
                ev = [P, ts.stop - ts.start, E]
                least = top8[:, ts, TOPK - 1:TOPK].to_broadcast(ev)
                dve.tensor_tensor(r_b[:, ts, :], r_a[:, ts, :], least, ALU.is_gt).then_inc(route, 1)
                step[0] += 1
                then(dve.tensor_tensor(biased[:, ts, :], r_a[:, ts, :], least, ALU.is_equal))
                dve.tensor_reduce(need[:, ts], r_b[:, ts, :], AX.X, ALU.add).then_inc(route, 1)
                step[0] += 1
                then(dve.tensor_tensor_scan(r_c[:, ts, :].rearrange("p t e -> p (t e)"),
                                            keep[:, ts, :].rearrange("p t e -> p (t e)"),
                                            biased[:, ts, :].rearrange("p t e -> p (t e)"), 0.0, ALU.mult, ALU.add))
                then(dve.tensor_tensor(r_c[:, ts, :], r_c[:, ts, :], need[:, ts].unsqueeze(2).to_broadcast(ev),
                                       ALU.add))

            def expert_weights(ts):
                ev = [P, ts.stop - ts.start, E]
                then(dve.tensor_scalar(r_c[:, ts, :], r_c[:, ts, :], TOPK + 0.5, None, ALU.is_lt))
                then(dve.tensor_tensor(r_c[:, ts, :], r_c[:, ts, :], biased[:, ts, :], ALU.mult))
                then(dve.tensor_tensor(r_b[:, ts, :], r_b[:, ts, :], r_c[:, ts, :], ALU.add))
                then(dve.tensor_tensor(r_b[:, ts, :], r_b[:, ts, :], score[:, ts, :], ALU.mult))
                then(dve.tensor_reduce(wsum[:, ts], r_b[:, ts, :], AX.X, ALU.add))
                then(dve.tensor_scalar(wsum[:, ts], wsum[:, ts], 1e-20, None, ALU.add))
                then(dve.reciprocal(wsum[:, ts], wsum[:, ts]))
                then(dve.tensor_scalar(wsum[:, ts], wsum[:, ts], 2.5, None, ALU.mult))
                dve.tensor_tensor(combine[:, ts, :], r_b[:, ts, :], wsum[:, ts].unsqueeze(2).to_broadcast(ev),
                                  ALU.mult).then_inc(comb_s, 1)

            parts = (group_scores, choose_groups, choose_experts, expert_weights)
            early, late = slice(0, NT - 3), slice(NT - 3, NT)

            dve.wait_ge(x_in_s[0], 16)
            norm_stats(0, 0)
            dve.wait_ge(x_in_s[1], 16)
            norm_stats(0, 1)
            norm_apply(0, 0)
            dve.memset(vbd[:, :, :, :, :, :], 0.0).then_inc(vbd_zero, 1)
            dve.wait_ge(vbd_zero, 1)
            for h in range(HR):
                dve.memset(vbd[QUAD * h:QUAD * (h + 1), :, :, :, h, HD:HD + 1], 1.0).then_inc(vbd_zero, 1)
            dve.wait_ge(headsel_r, 2)
            dve.tensor_reduce(hmask[:, :], headsel[:, :].rearrange("p (r h) -> p h r", r=NR), AX.X,
                              ALU.add).then_inc(hm_r, 1)
            dve.wait_ge(hm_r, 1)
            dve.tensor_scalar(hmask[:, :], hmask[:, :], float(HD) ** -0.5, None, ALU.mult).then_inc(hm_r, 1)
            for h in range(2):
                dve.memset(k2[DH * h:DH * (h + 1), :, :, 1 - h, :], 0.0).then_inc(k2_zero, 1)
            for i in range(STEPS):
                if 3 <= i <= NT:
                    residual1(i - 3)
                if i < NT:
                    build_vbd(i)
                if i + 1 < NT:
                    norm_apply(0, i + 1)
                if i == 0:
                    for t in range(2, NT):
                        dve.wait_ge(x_in_s[t], 16)
                        norm_stats(0, t)
                if 1 <= i < NT + 1:
                    mask1(i - 1)
                if 2 <= i < NT + 2:
                    norm_y(i - 2)
                if 1 <= i < NT + 1:
                    max1_sub(i - 1)
                if i == NT + 1:
                    softmax2_max(0)
                if 3 <= i <= NT:
                    norm_stats(1, i - 3)
                if NT <= i < NT + 2:
                    residual1(i - 2)
                    norm_stats(1, i - 2)
                if NT + 2 <= i < 2 * NT + 2:
                    softmax2_sum(i - NT - 2)
                if NT + 2 <= i < 2 * NT + 1:
                    softmax2_max(i - NT - 1)
                if NT + 4 <= i < 2 * NT + 2 or i == 2 * NT + 3:
                    split_x3(i - NT - 4)
                if NT + 3 <= i < 2 * NT + 3:
                    residual2(i - NT - 3)
                    norm_stats(2, i - NT - 3)
                if i == 2 * NT + 2:
                    split_x3(i - NT - 4)
                if i == 2 * NT + 1:
                    dve.wait_ge(zeroed, 8)
                    group_scores(early)
                if i == 2 * NT + 2:
                    choose_groups(early)

            def multiply(k, j):
                dve.wait_ge(sil_s, k + 1)
                dve.wait_ge(u_s, k + 1)
                if j >= 4:
                    dve.wait_ge(y_s, k - 3)
                dve.tensor_tensor(act[:, j % 4, :], sil[:, j % 2, :], bank[2 + j % 2], ALU.mult).then_inc(g_s, 1)

            def add_shared(c):
                dve.wait_ge(y_s, (NSH - 1) * NCH + c + 1)
                dve.tensor_tensor(x[:, c * TPC:(c + 1) * TPC, :].rearrange("p t d -> p (t d)"), bank[4 + c],
                                  x[:, c * TPC:(c + 1) * TPC, :].rearrange("p t d -> p (t d)"),
                                  ALU.add).then_inc(acc_s, TPC)

            def accumulate(k, j, e):
                c = j % NCH
                dve.wait_ge(y_s, k + 1)
                dve.wait_ge(acc_s, k * TPC - ACC_LAG)
                for m in range(TPC):
                    t = c * TPC + m
                    dve.scalar_tensor_tensor(out=x[:, t, :], in0=bank[4 + (j + 2) % 4][:, m * D:(m + 1) * D],
                                             scalar=combine[:, t, bass.ds(e, 1)], in1=x[:, t, :],
                                             op0=ALU.mult, op1=ALU.add).then_inc(acc_s, 1)

            rest = [(choose_experts, early), (expert_weights, early)] + [(part, late) for part in parts]
            for k in range(LEAD):
                if k < len(rest):
                    part, ts = rest[k]
                    part(ts)
                multiply(k, k)
                if k == len(rest) - 1:
                    dve.wait_ge(comb_s, 2)
                    for c in range(NCH):
                        add_shared(c)
                if k >= len(rest):
                    accumulate(k - 2, k - 2, (k - 2) // NCH - NSH)
            with dve.Fori(0, TURNS - 1) as it:
                for j in range(LEAD, LEAD + TURN):
                    multiply(it * TURN + j, j)
                    accumulate(it * TURN + (j - 2), j - 2, it * RING + ((j - 2) // NCH - NSH))
            for k in range(NK - TURN + LEAD - PEEL, NK):
                multiply(k, k)
                accumulate(k - 2, k - 2, (k - 2) // NCH - NSH)
            for k in range(NK - 2, NK):
                accumulate(k, k, k // NCH - NSH)

        @block.tensor
        def _(pe):
            def keep_busy(times):
                for _ in range(times):
                    pe.transpose(PV[:, 0:P], ident[:, :], ident[:, :])

            def transpose_xn(n, t, dst):
                pe.wait_ge(xn_s[n], t + 1)
                pe.transpose(dst, xn[:, n, t % 2, :], ident[:, :]).then_inc(xT_s[n], 1)

            def project_qkv(t):
                pe.wait_ge(xnT_s, t + 1)
                if t == 0:
                    pe.wait_ge(wqkv_l, 16)
                if t >= 1:
                    pe.wait_ge(qkn_s, 2 * t)
                pe.matmul(QK[:, 0:2 * D], xnT[:, t % 2, :], wqkv_sb[:, 0:2 * D],
                          start=True, stop=True).then_inc(qk_s, 1)

            def project_v(t):
                for h in range(HR):
                    wv = wqkv_sb[:, 2 * D:3 * D].rearrange("p (r h d) -> p r h d", r=NR, h=HR)[:, :, h, :]
                    for g in range(NG):
                        last = pe.matmul(T1[QUAD * h:QUAD * (h + 1), VCOL + QUAD * g:VCOL + QUAD * (g + 1)],
                                         xnT[:, t % 2, LS * g:LS * (g + 1)], wv, start=True, stop=True)
                last.then_inc(v_s, 1)

            def transpose_qk(t):
                pe.wait_ge(qkn_s, 2 * (t + 1))
                pe.wait_ge(vbd_s, t + 1)
                for n in range(2):
                    last = pe.transpose(T1[:, QKTCOL + n * P:QKTCOL + (n + 1) * P], qkn[:, t % 2, n, :], ident[:, :])
                last.then_inc(qkTp_s, 1)

            def scores1(t):
                pe.wait_ge(qkT_s, t + 1)
                pe.wait_ge(kbd_s, t + 1)
                if t >= 1:
                    pe.wait_ge(sm1_s, t)
                for g in range(NG):
                    for r in range(NR):
                        rows = slice(QUAD * r, QUAD * (r + 1))
                        last = pe.matmul(wide[QUAD * g:QUAD * (g + 1), r, 0:P],
                                         qkT[rows, t % 2, 0, LS * g:LS * (g + 1)],
                                         kbd[rows, t % 2, g, :, :].rearrange("p h k -> p (h k)"), start=True, stop=True)
                last.then_inc(S1_s, 1)

            def transpose_p1(t):
                pe.wait_ge(p1_s, t + 1)
                if t >= 1:
                    pe.wait_ge(res1_s, t)
                for r in range(NR):
                    last = pe.transpose(PV[:, r * P:(r + 1) * P], p1[:, t % 2, r * P:(r + 1) * P], ident[:, :])
                last.then_inc(p1T_s, 1)

            def values1(t):
                pe.wait_ge(p1Tc_s, t + 1)
                pe.wait_ge(vbd_s, t + 1)
                for r in range(NR):
                    for g in range(NG):
                        last = pe.matmul(PV[QUAD * g:QUAD * (g + 1), r * VA:(r + 1) * VA],
                                         p1T[:, r, LS * g:LS * (g + 1)],
                                         vbd[:, t % 3, g, r, :, :].rearrange("p h d -> p (h d)"), start=True, stop=True)
                last.then_inc(y1_s, 1)

            def project_y(t):
                pe.wait_ge(yn_s, t + 1)
                pe.transpose(PV[:, 2 * P:3 * P], yn[:, :, :].rearrange("p h d -> p (h d)"),
                             ident[:, :]).then_inc(yTp_s, 1)

            def project_out(t):
                if t == 0:
                    pe.wait_ge(wproj_l, 16)
                pe.wait_ge(yT_s, t + 1)
                pe.matmul(PV[:, 3 * P:4 * P], yT[:, :], wproj_sb[:, :], start=True, stop=True).then_inc(o1_s, 1)

            def fold(u, halves=(0, 1)):
                kind, j = u
                n = unit_no[u]
                dst = fold_bank(u)
                if halves[0] == 0 and kind == "VW" and j >= 1:
                    pe.wait_ge(f_copied, n - 1)
                elif halves[0] == 0 and n >= 1:
                    pe.wait_ge(f_copied, n)
                if kind == "ctx":
                    pe.wait_ge(ctx_l, 16)
                    for m in range(2):
                        last = pe.transpose(FOLD[:, m * P:(m + 1) * P], ctx_sb[:, m, :], ident[:, :])
                elif kind == "wq":
                    pe.wait_ge(wq_l, 16)
                    for m in range(2 * halves[0], 2 * halves[-1] + 2):
                        last = pe.transpose(FOLD[:, m * P:(m + 1) * P], wq_sb[:, (4 * j + m) * P:(4 * j + m + 1) * P],
                                            ident[:, :])
                elif kind == "kv":
                    pe.wait_ge(wkv_l, 16)
                    for m in range(2):
                        last = pe.matmul(FOLD[:, m * B * CTX:(m + 1) * B * CTX],
                                         wkv_sb[:, m * INNER + j * P:m * INNER + (j + 1) * P],
                                         ctxT[:, :, :].rearrange("p b s -> p (b s)"), start=True, stop=True)
                elif kind == "A":
                    pe.wait_ge(k2_zero, 2)
                    for m in halves:
                        bs = slice(m * B // 2, (m + 1) * B // 2)
                        last = pe.matmul(FOLD[:, m * B * CTX:(m + 1) * B * CTX], wqT[:, j, :],
                                         k2[:, j % 2, bs, :, :].rearrange("p b h s -> p (b h s)"),
                                         start=True, stop=True)
                else:
                    pe.wait_ge(wout_l, 16)
                    if j == 1:
                        pe.wait_ge(qkn_s, 2 * NT)
                    for b in range(B):
                        last = pe.matmul(dst[:, b * D:(b + 1) * D], v2[:, j, b, :, :].rearrange("p h s -> p (h s)"),
                                         wout_sb[:, j, :], start=True, stop=True)
                if halves[-1] == 1:
                    last.then_inc(f_ready, 1)

            def scores2(t):
                b = t // TPB
                pe.wait_ge(xn2T_s, t + 1)
                if t == 0:
                    pe.wait_ge(sm1_s, NT)
                    pe.wait_ge(f_copied, unit_no[("A", NPAIR - 1)] + 1)
                if t >= 2:
                    pe.wait_ge(sub2_s, t - 1)
                fold_b = qk_fold[:, b, :, :].rearrange("p j s -> p (j s)")
                for n in range(2):
                    last = pe.matmul(wide[:, 2 * (t % 2) + n, :], xn2T[:, t % 2, :], fold_b[:, n * 512:(n + 1) * 512],
                                     start=True, stop=True)
                last.then_inc(S2_s, 1)

            def transpose_p2(t):
                pe.wait_ge(pn2_s, t + 1)
                if t == 0:
                    pe.wait_ge(res1_s, NT)
                    pe.wait_ge(f_copied, len(units))
                if t >= 1:
                    pe.wait_ge(p2Tc_s, 2 * t)
                for n in range(2):
                    for j in range(4):
                        m = 2 * (4 * n + j)
                        last = pe.transpose(PT2[n][:, j * P:(j + 1) * P],
                                            p2[:, t % 3, m:m + 2, :].rearrange("p h k -> p (h k)"), ident[:, :])
                    last.then_inc(p2T_s, 1)

            def output2(t, half_no):
                b = t // TPB
                pe.wait_ge(p2Tc_s, 2 * t + half_no + 1)
                if half_no == 0:
                    if t == 0:
                        pe.wait_ge(bo_r, 2)
                    if t >= 1:
                        pe.wait_ge(res2_s, t)
                    pe.matmul(OUT2[:, 0:D], ones_row[:, :], bias_out[:, :], start=True, stop=False)
                for j in range(half_no * NPAIR // 2, (half_no + 1) * NPAIR // 2):
                    last = pe.matmul(OUT2[:, 0:D], p2T[:, j, :], vo_fold[:, j, b, :],
                                     start=False, stop=(j == NPAIR - 1))
                if half_no == 1:
                    last.then_inc(o2_s, 1)

            def logits(t):
                pe.wait_ge(x3T_s, t + 1)
                pe.matmul(T1[:, 2 * P:2 * P + E], x3T[:, t % 2, :], rwT[:, :], start=True, stop=True).then_inc(lg_s, 1)

            def gate_up(k, j, n):
                c = j % NCH
                slot = (j // NCH) % RING
                pe.wait_ge(wsplit_lo, n + 1)
                if j < NCH:
                    pe.wait_ge(x3lo_s, TPC * (c + 1))
                if j == 0:
                    pe.wait_ge(sub2_s, NT)
                if j >= 2:
                    pe.wait_ge(g_s, k - 1)
                cols = slice(c * CHUNK, (c + 1) * CHUNK)
                h, u = bank[j % 2], bank[2 + j % 2]
                pe.matmul(h, gu_lo[:, slot, 0, :], x3hi[:, cols], start=True, stop=False)
                pe.matmul(h, gu_hi[:, slot, 0, :], x3lo[:, cols], start=False, stop=False)
                pe.matmul(h, gu_hi[:, slot, 0, :], x3hi[:, cols], start=False, stop=True).then_inc(h_s, 1)
                pe.matmul(u, gu_lo[:, slot, 1, :], x3hi[:, cols], start=True, stop=False)
                pe.matmul(u, gu_hi[:, slot, 1, :], x3lo[:, cols], start=False, stop=False)
                pe.matmul(u, gu_hi[:, slot, 1, :], x3hi[:, cols], start=False, stop=True).then_inc(u_s, 1)

            pe.wait_ge(ident_r, 1)
            keep_busy(14)
            transpose_xn(0, 0, T1[:, 0:P])
            for i in range(NT):
                us = units_of(i)
                project_qkv(i)
                if i >= 3:
                    project_out(i - 3)
                project_v(i)
                fold(us[0])
                if i == 0:
                    keep_busy(10)
                if i >= 2:
                    transpose_p1(i - 2)
                if i >= 1:
                    scores1(i - 1)
                if i >= 2:
                    values1(i - 2)
                transpose_qk(i)
                fold(us[1], halves=(0,))
                if i + 1 < NT:
                    pe.wait_ge(qkT_s, i + 1)
                    transpose_xn(0, i + 1, T1[:, 0:P])
                fold(us[1], halves=(1,))
                if i >= 2:
                    project_y(i - 2)
                for u in us[2:]:
                    fold(u)

            for i in range(NT, STEPS):
                us = units_of(i)
                if i == NT:
                    project_out(NT - 3)
                if i < NT + 2:
                    transpose_p1(i - 2)
                if i == NT:
                    scores1(NT - 1)
                    pe.wait_ge(qkT_s, NT)
                if i == NT:
                    transpose_xn(1, 0, T1[:, 0:P])
                for u in us[0:1]:
                    fold(u)
                if i < NT + 2:
                    values1(i - 2)
                if NT + 3 <= i < 2 * NT + 3:
                    transpose_p2(i - NT - 3)
                if i < 2 * NT:
                    scores2(i - NT)
                if i < NT + 2:
                    project_y(i - 2)
                for u in us[1:2]:
                    fold(u)
                if i < NT + 2:
                    project_out(i - 2)
                for u in us[2:]:
                    fold(u)
                if 2 * NT <= i < 2 * NT + 3:
                    output2(i - NT - 3, 0)
                if NT + 4 <= i < 2 * NT + 4:
                    t = i - NT - 4
                    pe.wait_ge(xn2T_s, min(i - NT + 1, NT))
                    if t >= 1:
                        pe.wait_ge(eneg_s, t)
                    transpose_xn(2, t, T1[:, P:2 * P])
                if NT + 3 <= i < 2 * NT:
                    output2(i - NT - 3, 0)
                if NT + 4 <= i < 2 * NT:
                    logits(i - NT - 4)
                if i < 2 * NT - 1:
                    pe.wait_ge(xn2T_s, i - NT + 1)
                    if i == NT + 2:
                        pe.wait_ge(rwT_s, 1)
                    if i == NT + 1:
                        pe.wait_ge(rw_l, 16)
                        pe.transpose(T1[:, 3 * P:3 * P + E], rw_sb[:, :], ident[0:E, 0:E]).then_inc(rwT_p, 1)
                    transpose_xn(1, i - NT + 1, T1[:, 0:P])
                if NT + 3 <= i < 2 * NT + 3:
                    output2(i - NT - 3, 1)
                if 2 * NT <= i < 2 * NT + 4:
                    logits(i - NT - 4)
                if i == 2 * NT + 2:
                    gate_up(0, 0, 0)

            def down_shared(k):
                n, c = k // NCH, k % NCH
                pe.wait_ge(g_s, k + 1)
                if k == 0:
                    pe.wait_ge(dn_l, 32)
                    pe.wait_ge(eneg_s, NT)
                    pe.wait_ge(res2_s, NT)
                for m in range(TPC):
                    last = pe.matmul(bank[4 + c][:, m * D:(m + 1) * D], act[:, k, m * P:(m + 1) * P], dn_w[:, n, :],
                                     start=(n == 0 and m == 0), stop=(n == NSH - 1 and m == TPC - 1))
                last.then_inc(y_s, 1)

            def down(k, j, n):
                pe.wait_ge(g_s, k + 1)
                if j >= PEEL + 2:
                    pe.wait_ge(acc_s, k * TPC - ACC_LAG - 2 * TPC)
                for m in range(TPC):
                    last = pe.matmul(bank[4 + (j + 2) % 4][:, m * D:(m + 1) * D], act[:, j % 4, m * P:(m + 1) * P],
                                     dn_w[:, bass.ds(n, 1), :].rearrange("p o d -> p (o d)"), start=True, stop=True)
                last.then_inc(y_s, 1)

            for k in range(LEAD):
                if k > 0:
                    gate_up(k, k, k // NCH)
                if 2 <= k < PEEL + 2:
                    down_shared(k - 2)
                if k >= PEEL + 2:
                    down(k - 2, k - 2, (k - 2) // NCH)
            with pe.Fori(0, TURNS - 1) as it:
                for j in range(LEAD, LEAD + TURN):
                    gate_up(it * TURN + j, j, it * RING + j // NCH)
                    down(it * TURN + (j - 2), j - 2, it * RING + (j - 2) // NCH)
            for k in range(NK - TURN + LEAD - PEEL, NK):
                gate_up(k, k, k // NCH)
                down(k - 2, k - 2, (k - 2) // NCH)
            for k in range(NK - 2, NK):
                down(k, k, k // NCH)


_INS = ["x", "ctx_1024", "L0_attn_w_qkv", "L0_attn_ln_w", "L0_attn_w_proj", "L0_xattn_ln_gamma", "L0_xattn_ln_beta",
        "L0_xattn_w_q", "L0_xattn_w_kv", "L0_xattn_w_out", "L0_xattn_b_out", "L0_xattn_gate", "L0_ffn_router_w",
        "L0_ffn_bias", "L0_ffn_gate_w", "L0_ffn_up_w", "L0_ffn_down_w", "L0_ffn_sh_gate_w", "L0_ffn_sh_up_w",
        "L0_ffn_sh_down_w"]


def kernel(**inputs):
    import numpy as _np
    import concourse.bacc as _bacc
    from concourse import mybir as _mybir
    from concourse.bass_utils import run_bass_kernel_spmd as _run

    nc = _bacc.Bacc("TRN2", target_bir_lowering=False, num_devices=1)
    arrays, args = {}, []
    for name in _INS:
        a = _np.ascontiguousarray(inputs[name])
        arrays[f"in_{name}_dram"] = a
        args.append(nc.dram_tensor(f"in_{name}_dram", a.shape, _mybir.dt.from_np(a.dtype), kind="ExternalInput").ap())
    out = nc.dram_tensor("out_dram", inputs["x"].shape, F32, kind="ExternalOutput").ap()
    decoder_layer(nc, *args, out)
    r = _run(nc, [arrays], core_ids=[0])
    return r.results[0]["out_dram"]
```
